# Optimizing a Trainium2 kernel written in Bass

```python
import numpy as np
import jax
import jax.numpy as jnp

def _softmax(x, axis=-1):
    return jax.nn.softmax(x, axis=axis)

def _gelu(x):
    return jax.nn.gelu(x, approximate=True)

def _silu(x):
    return jax.nn.silu(x)

def _sigmoid(x):
    return jax.nn.sigmoid(x)

def _layernorm(x, axis=-1, eps=1e-05):
    m = jnp.mean(x, axis=axis, keepdims=True)
    v = jnp.var(x, axis=axis, keepdims=True)
    return (x - m) / jnp.sqrt(v + eps)

def _scatter_add(tgt, idx, src, axis=0):
    return tgt.at[idx].add(src)

def _segment_sum(src, seg, n):
    return jax.ops.segment_sum(src, seg, n)
kernel_name = 'mk_vit_tower_cls_d1_tok_img768_r4_767b96'

def setup_inputs(seed: int=0):
    np.random.seed(seed)
    _w = jnp.asarray

    def _rec_inputs():
        import jax
        import jax.numpy as jnp
        _rk = jax.random.key(seed)
        x = -0.00040386 + 0.999972 * jax.random.normal(jax.random.fold_in(_rk, 1), (64, 64, 64, 3), jnp.float32)
        cls_tok = 0.02 * jax.random.normal(jax.random.fold_in(_rk, 5), (1, 1, 192), jnp.float32)
        return (x, cls_tok)
    x, cls_tok = _rec_inputs()

    def _L0_tok_setup():
        import jax, jax.numpy as jnp
        import numpy as np
        IMG = 64
        PATCH = 16
        C = 3
        D = 192
        NP_ = (IMG // PATCH) ** 2
        B = 64

        def _patchify(x):
            Bn, H, Wd, Cn = x.shape
            hp, wp = (H // PATCH, Wd // PATCH)
            x = x.reshape(Bn, hp, PATCH, wp, PATCH, Cn)
            x = x.transpose(0, 1, 3, 2, 4, 5)
            return x.reshape(Bn, hp * wp, PATCH * PATCH * Cn)
        key = jax.random.key(seed)
        k1, k2, k3 = jax.random.split(key, 3)
        x = jax.random.normal(k1, (B, IMG, IMG, C), dtype=jnp.float32)
        patch_dim = C * PATCH * PATCH
        W = jax.random.normal(k2, (patch_dim, D), dtype=jnp.float32) / np.sqrt(patch_dim)
        b = jnp.zeros((D,), dtype=jnp.float32)
        pos_emb = jax.random.normal(k3, (NP_, D), dtype=jnp.float32) * 0.02
        return {'x': x, 'W': W, 'b': b, 'pos_emb': pos_emb}
    _L0_tok_all = _L0_tok_setup()
    _L0_tok_in = {k: v for k, v in _L0_tok_all.items() if k in ('W', 'b', 'pos_emb')}
    del _L0_tok_all

    def _L0_attn_setup():
        import jax, jax.numpy as jnp
        import numpy as np
        EMBED_DIM = 192
        NUM_HEADS = 12
        HEAD_DIM = EMBED_DIM // NUM_HEADS
        SCALING = HEAD_DIM ** (-0.5)
        B, N = (4, 512)
        key = jax.random.key(seed)
        k_x, k_wqkv, k_bqkv, k_wo, k_bo = jax.random.split(key, 5)
        s = EMBED_DIM ** (-0.5)
        return {'x_q': jax.random.normal(k_x, (B, N, EMBED_DIM), dtype=jnp.float32), 'w_qkv': jax.random.normal(k_wqkv, (3 * EMBED_DIM, EMBED_DIM), dtype=jnp.float32) * s, 'b_qkv': jax.random.normal(k_bqkv, (3 * EMBED_DIM,), dtype=jnp.float32) * s, 'w_out': jax.random.normal(k_wo, (EMBED_DIM, EMBED_DIM), dtype=jnp.float32) * s, 'b_out': jax.random.normal(k_bo, (EMBED_DIM,), dtype=jnp.float32) * s}
    _L0_attn_all = _L0_attn_setup()
    _L0_attn_in = {k: v for k, v in _L0_attn_all.items() if k in ('w_qkv', 'b_qkv', 'w_out', 'b_out')}
    del _L0_attn_all

    def _L0_ffn_setup():
        import jax, jax.numpy as jnp
        import numpy as np
        DEPTH = 11

        def _fff_forward(inputs, weights_in, weights_out, depth=DEPTH):
            B, S, _ = inputs.shape
            n_nodes = weights_in.shape[0]
            max_index = n_nodes - 1
            all_logits = jnp.einsum('bsd,nd->bsn', inputs, weights_in)

            def step(prev_idx, _):
                sel = jnp.clip(prev_idx, 0, max_index)
                logits = jnp.take_along_axis(all_logits, sel[..., None], axis=-1)[..., 0]
                new_idx = jnp.clip(2 * sel + 1 + (logits > 0).astype(sel.dtype), 0, max_index)
                return (new_idx, (logits, new_idx))
            idx0 = jnp.zeros((B, S), dtype=jnp.int32)
            _, (logits_seq, idx_seq) = jax.lax.scan(step, idx0, None, length=depth - 1)
            logits = jnp.concatenate([jnp.zeros((1, B, S), all_logits.dtype), logits_seq], axis=0)
            node_idx = jnp.concatenate([idx0[None], idx_seq], axis=0)
            act = jax.nn.gelu(logits, approximate=False)
            onehot = jax.nn.one_hot(node_idx, n_nodes, dtype=act.dtype)
            coeff = jnp.einsum('dbs,dbsn->bsn', act, onehot)
            return jnp.einsum('bsn,nd->bsd', coeff, weights_out)
        key = jax.random.key(seed)
        k1, k2, k3 = jax.random.split(key, 3)
        B, S, D = (4, 1024, 192)
        n_nodes = 2 * DEPTH - 1
        return {'inputs': jax.random.normal(k1, (B, S, D), dtype=jnp.float32), 'weights_in': jax.random.normal(k2, (n_nodes, D), dtype=jnp.float32), 'weights_out': jax.random.normal(k3, (n_nodes, D), dtype=jnp.float32)}
    _L0_ffn_all = _L0_ffn_setup()
    _L0_ffn_in = {k: v for k, v in _L0_ffn_all.items() if k in ('weights_in', 'weights_out')}
    del _L0_ffn_all
    return {'x': x, 'cls_tok': cls_tok, 'L0_tok_W': _L0_tok_in['W'], 'L0_tok_b': _L0_tok_in['b'], 'L0_tok_pos_emb': _L0_tok_in['pos_emb'], 'L0_attn_w_qkv': _L0_attn_in['w_qkv'], 'L0_attn_b_qkv': _L0_attn_in['b_qkv'], 'L0_attn_w_out': _L0_attn_in['w_out'], 'L0_attn_b_out': _L0_attn_in['b_out'], 'L0_ffn_weights_in': _L0_ffn_in['weights_in'], 'L0_ffn_weights_out': _L0_ffn_in['weights_out']}

def reference(x, cls_tok, L0_tok_W, L0_tok_b, L0_tok_pos_emb, L0_attn_w_qkv, L0_attn_b_qkv, L0_attn_w_out, L0_attn_b_out, L0_ffn_weights_in, L0_ffn_weights_out):
    import jax
    import jax.numpy as jnp

    def _L0_tok_ref(x, W, b, pos_emb):
        import jax, jax.numpy as jnp
        import numpy as np
        IMG = 64
        PATCH = 16
        C = 3
        D = 192
        NP_ = (IMG // PATCH) ** 2
        B = 64

        def _patchify(x):
            Bn, H, Wd, Cn = x.shape
            hp, wp = (H // PATCH, Wd // PATCH)
            x = x.reshape(Bn, hp, PATCH, wp, PATCH, Cn)
            x = x.transpose(0, 1, 3, 2, 4, 5)
            return x.reshape(Bn, hp * wp, PATCH * PATCH * Cn)
        patches = _patchify(x)
        proj = jnp.einsum('bnd,de->bne', patches, W) + b
        return proj + pos_emb[None, :, :]

    def _L0_attn_ref(x_q, w_qkv, b_qkv, w_out, b_out):
        import jax, jax.numpy as jnp
        import numpy as np
        EMBED_DIM = 192
        NUM_HEADS = 12
        HEAD_DIM = EMBED_DIM // NUM_HEADS
        SCALING = HEAD_DIM ** (-0.5)
        B, N = (4, 512)
        b_sz, n, _ = x_q.shape
        qkv = jnp.einsum('bne,fe->bnf', x_q, w_qkv) + b_qkv
        qkv = qkv.reshape(b_sz, n, 3, NUM_HEADS, HEAD_DIM).transpose(0, 3, 2, 1, 4)
        q, k, v = (qkv[:, :, 0], qkv[:, :, 1], qkv[:, :, 2])
        q = q * SCALING
        attn = jnp.einsum('bhqd,bhkd->bhqk', q, k) + 1.0
        attn = jax.nn.softmax(attn, axis=-1)
        out = jnp.einsum('bhqk,bhkd->bhqd', attn, v)
        out = out.transpose(0, 2, 1, 3).reshape(b_sz, n, EMBED_DIM)
        return jnp.einsum('bne,fe->bnf', out, w_out) + b_out

    def _L0_ffn_ref(inputs, weights_in, weights_out):
        import jax, jax.numpy as jnp
        import numpy as np
        DEPTH = 11

        def _fff_forward(inputs, weights_in, weights_out, depth=DEPTH):
            B, S, _ = inputs.shape
            n_nodes = weights_in.shape[0]
            max_index = n_nodes - 1
            all_logits = jnp.einsum('bsd,nd->bsn', inputs, weights_in)

            def step(prev_idx, _):
                sel = jnp.clip(prev_idx, 0, max_index)
                logits = jnp.take_along_axis(all_logits, sel[..., None], axis=-1)[..., 0]
                new_idx = jnp.clip(2 * sel + 1 + (logits > 0).astype(sel.dtype), 0, max_index)
                return (new_idx, (logits, new_idx))
            idx0 = jnp.zeros((B, S), dtype=jnp.int32)
            _, (logits_seq, idx_seq) = jax.lax.scan(step, idx0, None, length=depth - 1)
            logits = jnp.concatenate([jnp.zeros((1, B, S), all_logits.dtype), logits_seq], axis=0)
            node_idx = jnp.concatenate([idx0[None], idx_seq], axis=0)
            act = jax.nn.gelu(logits, approximate=False)
            onehot = jax.nn.one_hot(node_idx, n_nodes, dtype=act.dtype)
            coeff = jnp.einsum('dbs,dbsn->bsn', act, onehot)
            return jnp.einsum('bsn,nd->bsd', coeff, weights_out)
        return _fff_forward(inputs, weights_in, weights_out)
    h = _L0_tok_ref(x, L0_tok_W, L0_tok_b, L0_tok_pos_emb)
    h = jnp.concatenate([jnp.broadcast_to(cls_tok, (h.shape[0], 1, h.shape[2])), h], axis=1)
    h = h + _L0_attn_ref(_layernorm(h, axis=-1), L0_attn_w_qkv, L0_attn_b_qkv, L0_attn_w_out, L0_attn_b_out)
    h = h + _L0_ffn_ref(_layernorm(h, axis=-1), L0_ffn_weights_in, L0_ffn_weights_out)
    return h

_drawn_inputs = setup_inputs


def setup_inputs(seed=0):
    import zlib

    import numpy as np

    out = dict(_drawn_inputs(seed))
    spreads = {'L0_tok_b': (0.0, 0.1)}
    factors = {}
    for name, (base, spread) in spreads.items():
        noise = np.random.default_rng([zlib.crc32(name.encode()), seed]).standard_normal(out[name].shape)
        drawn = base * np.exp(spread * noise) if base else spread * noise
        out[name] = jnp.asarray(drawn.astype(out[name].dtype))
    for name, factor in factors.items():
        out[name] = (out[name] * factor).astype(out[name].dtype)
    return out
```

```python
import numpy as np
import concourse.bass as bass
from concourse import mybir
from contextlib import ExitStack

B, NP, D, PD = 64, 16, 192, 768
NT = NP + 1
H, HD = 12, 16
NODES = 21
NI = 9
P = 128
ST = 4
SB = B // ST
SC = SB * NT
KC = PD // P
C = D // 2
HC = H // 2
KR = NT * HC
QPAD = SC + 16
HA, HB = 8, 4
TILES = B * NP // P
ALLT = TILES + 1
EPS = 1e-5
SCALING = HD ** -0.5


def vit_block(nc, xt, w_tok, posb, w_qkv, b_qkv, w_out, bv, bo, cls_tok, w_in, w_node, masks, ident_d,
              out_patch, out_cls):
    fp32 = mybir.dt.float32
    ALU = mybir.AluOpType
    ACT = mybir.ActivationFunctionType
    AX = mybir.AxisListType

    v_scratch = nc.dram_tensor("v_scratch", (2, B, NP, C), fp32, kind="Internal").ap()
    vcls_scratch = nc.dram_tensor("vcls_scratch", (2, C), fp32, kind="Internal").ap()

    ctx = ExitStack()
    with ctx:
        def sb(name, shape):
            return ctx.enter_context(nc.sbuf_tensor(name, shape, fp32))

        def sem(name):
            return ctx.enter_context(nc.semaphore(name))

        wtok = sb("wtok", [P, KC, D])
        wqkv = sb("wqkv", [C, 2, 3 * D])
        wout = sb("wout", [C, 2, D])
        win = sb("win", [C, 2, NODES])
        wnode = sb("wnode", [NODES, D])
        pos = sb("pos", [P, 3, D])
        posbias = sb("posbias", [P, 2, D])
        bqk = sb("bqk", [P, 4])
        bqs = sb("bqs", [P, 2])
        bvc = sb("bvc", [C, 2])
        bob = sb("bob", [P, D])
        mask = sb("mask", [P, HA + HC])
        ident = sb("ident", [P, P])
        mhalf = sb("mhalf", [P, 2])
        x_sb = sb("x_sb", [P, ST, KC, SB * NP])
        h = sb("h", [P, ALLT, D])
        hb = sb("hb", [P, ALLT, D])
        h2 = sb("h2", [P, ALLT, D])
        fin = sb("fin", [P, ALLT, D])
        hn = sb("hn", [P, 2, 2, D])
        h2n = sb("h2n", [P, 3, D])
        stats = sb("stats", [P, 3, 6])
        mv = sb("mv", [P, ALLT, 2])
        ve = sb("ve", [P, ALLT])
        rstd = sb("rstd", [P, ALLT])
        mv2 = sb("mv2", [P, ALLT, 2])
        ve2 = sb("ve2", [P, ALLT])
        rstd2 = sb("rstd2", [P, ALLT])
        hnT = sb("hnT", [C, 2, ST, NT, SB])
        qa = sb("qa", [P, ST, QPAD])
        qb = sb("qb", [64, ST, QPAD])
        ka = sb("ka", [P, 2, SC])
        kb = sb("kb", [64, 2, SC])
        kda = sb("kda", [P, 2, HA, SC])
        kdb = sb("kdb", [64, 2, HB, SC])
        v_sb = sb("v_sb", [P, 2, 2, D])
        vcls = sb("vcls", [1, D])
        vc = sb("vc", [KR, 2, B, HD])
        vd = sb("vd", [KR, 2, 2, SB, C])
        smax = sb("smax", [P, 2, 24])
        dif = sb("dif", [P, 2, 2 * H * NT])
        ex = sb("ex", [P, 2, 2 * H * NT])
        rsum = sb("rsum", [P, 2, 24])
        rinv = sb("rinv", [P, 2, 24])
        prob = sb("prob", [P, 2, 4, KR])
        pT = sb("pT", [KR, 2, 4, 4, NT])
        oT = sb("oT", [C, 2, ST, NP, SB])
        oTc = sb("oTc", [C, 2, B])
        h2T = sb("h2T", [C, 2, 3, P])
        logit = sb("logit", [P, ALLT, NODES])
        gel = sb("gel", [P, ALLT, NODES])
        side = sb("side", [P, ALLT, NI + 1, 2])
        path = sb("path", [P, ALLT, NODES])
        act = sb("act", [P, ALLT, NODES])
        coef = sb("coef", [P, ALLT, NODES])
        r20 = sb("r20", [P, ALLT, 4])
        cT = sb("cT", [NODES, ALLT, P])

        bank = [ctx.enter_context(nc.psum_tensor(f"bank{i}", [P, 512], fp32)) for i in range(8)]
        tokB = bank[0][:, 0:2 * D].rearrange("p (t d) -> p t d", t=2)
        trB = bank[1]
        qaB, kaB, qkbB = bank[2], bank[3], bank[4]
        oTB = [bank[2], bank[3]]
        scB = [bank[5], bank[6]]
        pTB = [bank[7], bank[4]]
        lgB = bank[7]
        finB = [bank[2], bank[3], bank[0], bank[2], bank[3]]

        in_x = [sem(f"in_x{s}") for s in range(ST)]
        in_wtok, in_ident, in_pos, in_cls, in_wqkv = sem("in_wtok"), sem("in_ident"), sem("in_pos"), sem("in_cls"), sem("in_wqkv")
        in_bqk, in_mask, in_wout, in_win, in_wnode = sem("in_bqk"), sem("in_mask"), sem("in_wout"), sem("in_win"), sem("in_wnode")
        in_bv, in_bo = sem("in_bv"), sem("in_bo")
        vcls_stored, v_stored = sem("vcls_stored"), sem("v_stored")
        vcls_back = sem("vcls_back")
        v_back = [sem(f"v_back{s}") for s in range(ST)]
        out_done = sem("out_done")
        pe_h, pe_hT, pe_qa, pe_ka, pe_qkb, pe_v = sem("pe_h"), sem("pe_hT"), sem("pe_qa"), sem("pe_ka"), sem("pe_qkb"), sem("pe_v")
        pe_sc, pe_pT, pe_oT, pe_o, pe_h2T, pe_lg = sem("pe_sc"), sem("pe_pT"), sem("pe_oT"), sem("pe_o"), sem("pe_h2T"), sem("pe_lg")
        pe_cT, pe_fin = sem("pe_cT"), sem("pe_fin")
        hT_copied, qa_copied, ka_copied, qkb_copied, v_copied = sem("hT_copied"), sem("qa_copied"), sem("ka_copied"), sem("qkb_copied"), sem("v_copied")
        exp_done, pT_copied, oT_copied, h2T_copied, lg_copied = sem("exp_done"), sem("pT_copied"), sem("oT_copied"), sem("h2T_copied"), sem("lg_copied")
        gelu_done, cT_copied, bqs_done = sem("gelu_done"), sem("cT_copied"), sem("bqs_done")
        h_added, hn_ready, ve_ready, dif_ready, prob_ready = sem("h_added"), sem("hn_ready"), sem("ve_ready"), sem("dif_ready"), sem("prob_ready")
        h2_added, h2n_ready, ve2_ready, coef_ready, fin_ready = sem("h2_added"), sem("h2n_ready"), sem("ve2_ready"), sem("coef_ready"), sem("fin_ready")
        dve_step = sem("dve_step")
        consts_set, rstd_ready, rstd2_ready, kd_ready, vd_ready, hb_ready = (
            sem("consts_set"), sem("rstd_ready"), sem("rstd2_ready"), sem("kd_ready"), sem("vd_ready"), sem("hb_ready"))

        block = ctx.enter_context(nc.Block())

        def rows(t):
            return P if t < TILES else B

        @block.sync
        def _(sp):
            sp.dma_start(wtok[:], w_tok).then_inc(in_wtok, 16)
            for s in range(ST):
                sp.dma_start(x_sb[:, s], xt[s]).then_inc(in_x[s], 16)
                if s == 0:
                    sp.dma_start(wqkv[:], w_qkv).then_inc(in_wqkv, 16)
            sp.dma_start(wout[:], w_out).then_inc(in_wout, 16)
            sp.dma_start(win[:], w_in).then_inc(in_win, 16)
            sp.dma_start(wnode[:], w_node).then_inc(in_wnode, 16)
            sp.wait_ge(v_copied, 1)
            sp.dma_start(vcls_scratch.rearrange("(a c) d -> a (c d)", a=1), vcls[:]).then_inc(vcls_stored, 16)
            sp.wait_ge(vcls_stored, 16)
            for c in range(2):
                src = vcls_scratch[c].rearrange("(h d) -> h d", d=HD).unsqueeze(1).to_broadcast([HC, B, HD])
                sp.dma_start(vc[0:HC, c], src).then_inc(vcls_back, 16)
            for s in range(ST):
                sp.wait_ge(v_copied, s + 2)
                for t in range(2):
                    for c in range(2):
                        dst = v_scratch[c, s * SB:(s + 1) * SB, 8 * t:8 * t + 8].rearrange("b n d -> n b d")
                        sp.dma_start(dst, v_sb[:, s % 2, t, c * C:(c + 1) * C]).then_inc(v_stored, 16)
                sp.wait_ge(v_stored, 64 * (s + 1))
                for c in range(2):
                    src = v_scratch[c, s * SB:(s + 1) * SB].rearrange("b n (h d) -> (n h) b d", d=HD)
                    sp.dma_start(vc[HC:KR, c, s * SB:(s + 1) * SB], src).then_inc(v_back[s], 16)
            stores = 0
            for g in range(ST):
                sp.wait_ge(fin_ready, g + 1)
                sp.dma_start(out_patch[:, 2 * g:2 * g + 2], fin[:, 2 * g:2 * g + 2]).then_inc(out_done, 16)
                stores += 16
            sp.wait_ge(fin_ready, ST + 1)
            sp.dma_start(out_cls, fin[0:B, TILES]).then_inc(out_done, 16)
            sp.wait_ge(out_done, stores + 16)

        @block.gpsimd
        def _(pool):
            pool.memset(mhalf[:], -0.5).then_inc(consts_set, 1)
            pool.memset(qa[:, :, SC:], 0.0).then_inc(consts_set, 1)
            pool.memset(qb[:, :, SC:], 0.0).then_inc(consts_set, 1)

            def root(n, t0, nt, r):
                pool.wait_ge(ve_ready, n + 1)
                pool.tensor_tensor(rstd[0:r, t0:t0 + nt], ve[0:r, t0:t0 + nt], mhalf[0:r, 0:nt], ALU.pow).then_inc(rstd_ready, 1)

            def root2(s):
                pool.wait_ge(ve2_ready, s + 1)
                nt = 2 if s < ST - 1 else 3
                for a, n, r in ((2 * s, 2, P), (TILES, 1, B))[0:nt - 1]:
                    pool.tensor_tensor(rstd2[0:r, a:a + n], ve2[0:r, a:a + n], mhalf[0:r, 0:n], ALU.pow).then_inc(rstd2_ready, 1)

            def add_bias_out(s):
                pool.wait_ge(h_added, s + 1)
                pool.tensor_tensor(hb[:, 2 * s:2 * s + 2], h[:, 2 * s:2 * s + 2], bob[:].unsqueeze(1).to_broadcast([P, 2, D]), ALU.add).then_inc(hb_ready, 1)

            def spread_keys(s):
                pool.wait_ge(ka_copied, s + 1)
                if s >= 2:
                    pool.wait_ge(pe_sc, 2 * (s - 1))
                pool.tensor_tensor(kda[:, s % 2], ka[:, s % 2].unsqueeze(1).to_broadcast([P, HA, SC]),
                                   mask[:, 0:HA].unsqueeze(2).to_broadcast([P, HA, SC]), ALU.mult).then_inc(kd_ready, 1)
                pool.wait_ge(qkb_copied, 2 * (s + 1))
                pool.tensor_tensor(kdb[:, s % 2], kb[:, s % 2].unsqueeze(1).to_broadcast([64, HB, SC]),
                                   mask[0:64, 0:HB].unsqueeze(2).to_broadcast([64, HB, SC]), ALU.mult).then_inc(kd_ready, 1)

            def spread_values(s):
                if s == 0:
                    pool.wait_ge(vcls_back, 32)
                pool.wait_ge(v_back[s], 32)
                if s >= 2:
                    pool.wait_ge(pe_oT, 2 * (s - 1))
                for c in range(2):
                    pool.tensor_tensor(vd[:, s % 2, c].rearrange("p b (h d) -> p b h d", d=HD),
                                       vc[:, c, s * SB:(s + 1) * SB].unsqueeze(2).to_broadcast([KR, SB, HC, HD]),
                                       mask[0:KR, HA:HA + HC].unsqueeze(1).unsqueeze(3).to_broadcast([KR, SB, HC, HD]),
                                       ALU.mult).then_inc(vd_ready, 1)

            pool.wait_ge(consts_set, 3)
            root(0, TILES, 1, B)
            root(1, 0, 2, P)
            pool.wait_ge(in_bo, 16)
            pool.wait_ge(in_cls, 16)
            pool.tensor_tensor(hb[0:B, TILES], h[0:B, TILES], bob[0:B], ALU.add).then_inc(hb_ready, 1)
            root(2, 2, 2, P)
            pool.wait_ge(in_mask, 16)
            spread_keys(0)
            root(3, 4, 2, P)
            add_bias_out(0)
            spread_values(0)
            spread_keys(1)
            root2(0)
            root(4, 6, 2, P)
            add_bias_out(1)
            spread_values(1)
            spread_keys(2)
            root2(1)
            add_bias_out(2)
            spread_values(2)
            spread_keys(3)
            root2(2)
            add_bias_out(3)
            spread_values(3)
            root2(3)

        @block.scalar
        def _(sc):
            sc.dma_start(ident[:], ident_d).then_inc(in_ident, 16)
            sc.dma_start(h[0:B, TILES], cls_tok.to_broadcast([B, D])).then_inc(in_cls, 16)
            sc.dma_start(pos[:], posb).then_inc(in_pos, 16)
            sc.dma_start(bqk[:], b_qkv).then_inc(in_bqk, 16)
            sc.dma_start(mask[:], masks).then_inc(in_mask, 16)
            sc.dma_start(bvc[:], bv).then_inc(in_bv, 16)
            sc.dma_start(bob[:], bo.to_broadcast([P, D])).then_inc(in_bo, 16)

            def copy_hT(s):
                sc.wait_ge(pe_hT, s + 2)
                if s >= 0:
                    src = trB[0:C, :].rearrange("p (c n b) -> p c n b", c=2, n=NP)
                    sc.activation(hnT[:, :, s, 1:NT], src, ACT.Copy).then_inc(hT_copied, 1)
                else:
                    sc.activation(hnT[:, :, :, 0], trB[0:C, 0:2 * B].rearrange("p (c s b) -> p c s b", c=2, s=ST), ACT.Copy).then_inc(hT_copied, 1)

            def by_image(ap):
                return ap.rearrange("p (n b) -> p b n", b=SB)

            def copy_qkv(s):
                if s == 0:
                    sc.wait_ge(bqs_done, 1)
                sc.wait_ge(pe_qa, s + 1)
                sc.activation(qa[:, s, 0:SC].rearrange("p (b n) -> p b n", n=NT), by_image(qaB[:, 0:SC]), ACT.Identity, bias=bqs[:, 0:1], scale=SCALING).then_inc(qa_copied, 1)
                sc.wait_ge(pe_ka, s + 1)
                if s >= 2:
                    sc.wait_ge(kd_ready, 2 * (s - 1))
                sc.activation(ka[:, s % 2].rearrange("p (b n) -> p b n", n=NT), by_image(kaB[:, 0:SC]), ACT.Identity, bias=bqk[:, 1:2]).then_inc(ka_copied, 1)
                sc.wait_ge(pe_qkb, s + 1)
                sc.activation(qb[:, s, 0:SC].rearrange("p (b n) -> p b n", n=NT), by_image(qkbB[0:64, 0:SC]), ACT.Identity, bias=bqs[0:64, 1:2], scale=SCALING).then_inc(qkb_copied, 1)
                sc.activation(kb[:, s % 2].rearrange("p (b n) -> p b n", n=NT), by_image(qkbB[64:P, 0:SC]), ACT.Identity, bias=bqk[0:64, 3:4]).then_inc(qkb_copied, 1)
                sc.wait_ge(pe_v, s + 2)
                if s >= 2:
                    sc.wait_ge(v_stored, 64 * (s - 1))
                sc.activation(v_sb[:, s % 2], trB[:, 0:2 * D].rearrange("p (t d) -> p t d", t=2), ACT.Copy).then_inc(v_copied, 1)

            def exps(s):
                for i in range(2):
                    sc.wait_ge(dif_ready, 2 * s + i + 1)
                    if s:
                        sc.wait_ge(prob_ready, 2 * s + i - 1)
                    sc.activation(ex[:, i], dif[:, i], ACT.Exp, bias=mone).then_inc(exp_done, 1)

            def copy_pT(s):
                for i in range(2):
                    sc.wait_ge(pe_pT, 2 * s + i + 1)
                    src = pTB[i][0:KR, :].rearrange("p (g j q) -> p g j q", g=4, q=32)[:, :, :, 0:NT]
                    if s:
                        sc.wait_ge(pe_oT, 2 * s)
                    sc.activation(pT[:, i], src, ACT.Copy).then_inc(pT_copied, 1)

            def copy_oT(s):
                for c in range(2):
                    sc.wait_ge(pe_oT, 2 * s + 1 + c)
                    src = oTB[c][0:C, 0:SC].rearrange("p (b n) -> p n b", n=NT)
                    sc.activation(oT[:, c, s], src[:, 1:NT], ACT.Identity, bias=bvc[:, c:c + 1])
                    sc.activation(oTc[:, c, s * SB:(s + 1) * SB], src[:, 0], ACT.Identity, bias=bvc[:, c:c + 1]).then_inc(oT_copied, 1)

            def copy_h2T(s):
                sc.wait_ge(pe_h2T, s + 1)
                if s:
                    sc.wait_ge(pe_lg, s)
                sc.activation(h2T[:, :, 0:2], trB[0:C, :].rearrange("p (c t q) -> p c t q", c=2, q=P), ACT.Copy).then_inc(h2T_copied, 1)

            def copy_logits(s):
                sc.wait_ge(pe_lg, s + 1)
                nt = 2
                sc.activation(logit[:, 2 * s:2 * s + nt], lgB[:, 0:nt * NODES].rearrange("p (t n) -> p t n", n=NODES), ACT.Copy).then_inc(lg_copied, 1)

            mone = -1.0
            sc.wait_ge(in_bqk, 16)
            sc.activation(bqs[:], bqk[:].rearrange("p (a b) -> p b a", b=2)[:, 0], ACT.Copy, scale=SCALING).then_inc(bqs_done, 1)
            sc.wait_ge(in_bv, 16)
            copy_hT(-1)
            sc.wait_ge(pe_v, 1)
            sc.activation(vcls[:], bank[4][0:1, 0:D], ACT.Copy).then_inc(v_copied, 1)
            copy_hT(0)
            copy_qkv(0)
            for s in range(ST):
                if s:
                    copy_h2T(s - 1)
                    copy_logits(s - 1)
                if s < ST - 1:
                    copy_hT(s + 1)
                exps(s)
                if s < ST - 1:
                    copy_qkv(s + 1)
                else:
                    sc.wait_ge(lg_copied, ST - 1)
                    sc.activation(gel[:, 0:6], logit[:, 0:6], ACT.Gelu).then_inc(gelu_done, 1)
                copy_pT(s)
                copy_oT(s)
            for i, (t0, nt) in enumerate(((0, 4), (4, 2))):
                sc.wait_ge(pe_cT, i + 1)
                sc.activation(cT[:, t0:t0 + nt], bank[(4, 5)[i]][0:NODES, 0:nt * P].rearrange("p (t q) -> p t q", q=P), ACT.Copy).then_inc(cT_copied, 1)
            sc.wait_ge(pe_h2T, ST)
            sc.activation(h2T[:, :, 0:2], trB[0:C, :].rearrange("p (c t q) -> p c t q", c=2, q=P), ACT.Copy).then_inc(h2T_copied, 1)
            sc.wait_ge(pe_h2T, ST + 1)
            sc.activation(h2T[:, :, 2, 0:B], bank[6][0:C, 0:2 * B].rearrange("p (c q) -> p c q", c=2), ACT.Copy).then_inc(h2T_copied, 1)
            for i, (t0, nt, r) in enumerate(((6, 2, P), (8, 1, B))):
                sc.wait_ge(pe_lg, ST + i)
                src = lgB[0:r, 64 * i:64 * i + nt * NODES].rearrange("p (t n) -> p t n", n=NODES)
                sc.activation(logit[0:r, t0:t0 + nt], src, ACT.Copy).then_inc(lg_copied, 1)
                sc.activation(gel[0:r, t0:t0 + nt], src, ACT.Gelu).then_inc(gelu_done, 1)
            sc.wait_ge(pe_cT, 3)
            sc.activation(cT[:, 6:9], bank[4][0:NODES, 0:3 * P].rearrange("p (t q) -> p t q", q=P), ACT.Copy).then_inc(cT_copied, 1)

        @block.vector
        def _(dve):
            steps = [0]

            def after(ins):
                steps[0] += 1
                ins.then_inc(dve_step, 1)
                dve.wait_ge(dve_step, steps[0])

            def layernorm(src, tiles, mv_, ve_, rstd_, ve_sem, rstd_sem, rstd_at, dst, dst_sem):
                for i, t in enumerate(tiles):
                    r = rows(t)
                    last = dve.bn_stats(stats[0:r, i], src[0:r, t])
                after(last)
                for i, t in enumerate(tiles):
                    last = dve.bn_aggr(mv_[0:rows(t), t], stats[0:rows(t), i])
                after(last)
                for i, t in enumerate(tiles):
                    last = dve.tensor_scalar(ve_[0:rows(t), t:t + 1], mv_[0:rows(t), t, 1:2], EPS, None, ALU.add)
                last.then_inc(ve_sem, 1)
                dve.wait_ge(rstd_sem, rstd_at)
                for i, t in enumerate(tiles):
                    r = rows(t)
                    last = dve.tensor_scalar(dst[0:r, i], src[0:r, t], mv_[0:r, t, 0:1], rstd_[0:r, t:t + 1], ALU.subtract, ALU.mult)
                last.then_inc(dst_sem, 1)

            def embed(s):
                dve.wait_ge(pe_h, s + 1)
                dve.tensor_tensor(h[:, 2 * s:2 * s + 2], tokB, posbias[:], ALU.add).then_inc(h_added, 1)
                dve.wait_ge(h_added, s + 1)
                if s >= 2:
                    dve.wait_ge(pe_hT, s)
                layernorm(h, (2 * s, 2 * s + 1), mv, ve, rstd, ve_ready, rstd_ready, s + 2, hn[:, s % 2], hn_ready)

            def softmax(s):
                for i in range(2):
                    dve.wait_ge(pe_sc, 2 * s + i + 1)
                    scores = scB[i][:, 0:2 * H * NT].rearrange("p (h k) -> p h k", k=NT)
                    after(dve.tensor_reduce(out=smax[:, i], in_=scores, axis=AX.X, op=ALU.max))
                    if s:
                        dve.wait_ge(exp_done, 2 * s + i - 1)
                    dve.scalar_tensor_tensor(out=dif[:, i].rearrange("p (h k) -> p h k", k=NT), in0=scores, scalar=1.0,
                                             in1=smax[:, i].unsqueeze(2).to_broadcast([P, 2 * H, NT]),
                                             op0=ALU.add, op1=ALU.subtract).then_inc(dif_ready, 1)
                for i in range(2):
                    dve.wait_ge(exp_done, 2 * s + i + 1)
                    e3 = ex[:, i].rearrange("p (h k) -> p h k", k=NT)
                    after(dve.tensor_reduce(out=rsum[:, i], in_=e3, axis=AX.X, op=ALU.add))
                    after(dve.reciprocal(rinv[:, i], rsum[:, i]))
                    if s:
                        dve.wait_ge(pe_pT, 2 * (s - 1) + i + 1)
                    dve.tensor_tensor(prob[:, i].rearrange("p g (k h) -> p g h k", h=HC),
                                      ex[:, i].rearrange("p (g h k) -> p g h k", g=4, k=NT),
                                      rinv[:, i].rearrange("p (g h) -> p g h", g=4).unsqueeze(3).to_broadcast([P, 4, HC, NT]),
                                      ALU.mult).then_inc(prob_ready, 1)

            def residual(s):
                dve.wait_ge(pe_o, s + 1)
                dve.wait_ge(hb_ready, s + 2)
                dve.tensor_tensor(h2[:, 2 * s:2 * s + 2], tokB, hb[:, 2 * s:2 * s + 2], ALU.add).then_inc(h2_added, 1)
                if s == ST - 1:
                    dve.wait_ge(pe_o, s + 2)
                    dve.tensor_tensor(h2[0:B, TILES], bank[5][0:B, 0:D], hb[0:B, TILES], ALU.add).then_inc(h2_added, 1)
                    dve.wait_ge(h2_added, s + 2)
                else:
                    dve.wait_ge(h2_added, s + 1)
                if s:
                    dve.wait_ge(pe_h2T, s)
                tiles = (2 * s, 2 * s + 1) if s < ST - 1 else (2 * s, 2 * s + 1, TILES)
                layernorm(h2, tiles, mv2, ve2, rstd2, ve2_ready, rstd2_ready, s + 1 if s < ST - 1 else s + 2, h2n, h2n_ready)

            def tree(r, t0, nt, gelus):
                T = slice(t0, t0 + nt)
                lg = logit[0:r, T, 0:NI + 1]
                dve.tensor_scalar(side[0:r, T, :, 0], lg, 0.0, None, ALU.is_le)
                dve.tensor_scalar(side[0:r, T, :, 1], lg, 0.0, None, ALU.is_gt)
                dve.memset(path[0:r, T, 0:1], 1.0)
                after(dve.memset(coef[0:r, T, 0:1], 0.0))

                def down(dst, src, a, n):
                    return dve.tensor_tensor(dst[0:r, T, 2 * a + 1:2 * (a + n) + 1].rearrange("p t (n e) -> p t n e", e=2),
                                             src[0:r, T, a:a + n].unsqueeze(3).to_broadcast([r, nt, n, 2]),
                                             side[0:r, T, a:a + n], ALU.mult)
                after(down(path, path, 0, 1))
                after(down(path, path, 1, 2))
                after(down(path, path, 3, 4))
                after(down(path, path, 7, 3))
                after(dve.tensor_reduce(out=r20[0:r, T, 0], in_=path[0:r, T, 15:20], axis=AX.X, op=ALU.add))
                dve.tensor_scalar(path[0:r, T, 20], r20[0:r, T, 0], -1.0, 6.0, ALU.mult, ALU.add).then_inc(dve_step, 1)
                steps[0] += 1
                dve.wait_ge(dve_step, steps[0])
                dve.wait_ge(gelu_done, gelus)
                after(dve.tensor_tensor(act[0:r, T], path[0:r, T], gel[0:r, T], ALU.mult))
                after(down(coef, act, 0, NI + 1))
                after(dve.tensor_reduce(out=r20[0:r, T, 1], in_=act[0:r, T, 10:21], axis=AX.X, op=ALU.add))
                dve.tensor_tensor(coef[0:r, T, 20], coef[0:r, T, 20], r20[0:r, T, 1], ALU.add).then_inc(coef_ready, 1)

            dve.wait_ge(in_cls, 16)
            dve.wait_ge(consts_set, 3)
            layernorm(h, (TILES,), mv, ve, rstd, ve_ready, rstd_ready, 1, hn[:, 1], hn_ready)
            dve.wait_ge(in_pos, 16)
            after(dve.tensor_tensor(posbias[:], pos[:, 0:2], pos[:, 2:3].to_broadcast([P, 2, D]), ALU.add))
            embed(0)
            dve.wait_ge(pe_hT, 1)
            embed(1)
            embed(2)
            softmax(0)
            residual(0)
            embed(3)
            softmax(1)
            residual(1)
            softmax(2)
            residual(2)
            softmax(3)
            dve.wait_ge(lg_copied, ST - 1)
            tree(P, 0, 6, 1)
            residual(3)

            def finish(g):
                dve.wait_ge(pe_fin, g + 1)
                if g < ST:
                    dve.tensor_tensor(fin[:, 2 * g:2 * g + 2], finB[g][:, 0:2 * D].rearrange("p (t d) -> p t d", t=2),
                                      h2[:, 2 * g:2 * g + 2], ALU.add).then_inc(fin_ready, 1)
                else:
                    dve.tensor_tensor(fin[0:B, TILES], finB[g][0:B, 0:D], h2[0:B, TILES], ALU.add).then_inc(fin_ready, 1)
            for g in range(3):
                finish(g)
            dve.wait_ge(lg_copied, ST)
            tree(P, 6, 2, 2)
            dve.wait_ge(lg_copied, ST + 1)
            tree(B, 8, 1, 3)
            finish(3)
            finish(4)

        @block.tensor
        def _(pe):
            def project_patches(s):
                pe.wait_ge(in_x[s], 16)
                if s == 0:
                    pe.wait_ge(in_wtok, 16)
                elif s < ST - 1:
                    pe.wait_ge(h_added, s)
                else:
                    pe.wait_ge(h2_added, 1)
                for t in range(2):
                    for k in range(KC):
                        last = pe.matmul(tokB[:, t], x_sb[:, s, k, t * P:(t + 1) * P], wtok[:, k], start=(k == 0), stop=(k == KC - 1))
                last.then_inc(pe_h, 1)

            def turn_hn(s):
                pe.wait_ge(hn_ready, s + 2)
                if s == 0:
                    pe.wait_ge(hT_copied, 1)
                elif s == 1:
                    pe.wait_ge(v_copied, 2)
                else:
                    pe.wait_ge(h2T_copied, s - 1)
                for c in range(2):
                    for t in range(2):
                        last = pe.transpose(trB[0:C, (2 * c + t) * P:(2 * c + t + 1) * P], hn[:, s % 2, t, c * C:(c + 1) * C], ident[:])
                last.then_inc(pe_hT, 1)

            def qkv(s):
                pe.wait_ge(hT_copied, s + 2)
                if s == 0:
                    pe.wait_ge(in_wqkv, 16)
                for dst, col, done in ((qaB, 0, pe_qa), (kaB, 1, pe_ka), (qkbB, 2, pe_qkb)):
                    if dst is qkbB:
                        if s == 0:
                            pe.wait_ge(v_copied, 1)
                        elif s == 1:
                            pe.wait_ge(qkb_copied, 2)
                        else:
                            pe.wait_ge(pT_copied, 2 * (s - 1))
                    elif s == 1:
                        pe.wait_ge(qa_copied if dst is qaB else ka_copied, 1)
                    elif s:
                        pe.wait_ge(oT_copied, 2 * (s - 1))
                    for c in range(2):
                        last = pe.matmul(dst[:, 0:SC], wqkv[:, c, col * P:(col + 1) * P],
                                         hnT[:, c, s].rearrange("p n b -> p (n b)"), start=(c == 0), stop=(c == 1))
                    last.then_inc(done, 1)
                for t in range(2):
                    for c in range(2):
                        last = pe.matmul(trB[:, t * D:(t + 1) * D], hnT[:, c, s, 1 + 8 * t:9 + 8 * t].rearrange("p n b -> p (n b)"), wqkv[:, c, 2 * D:3 * D],
                                         start=(c == 0), stop=(c == 1))
                last.then_inc(pe_v, 1)

            def scores(s):
                pe.wait_ge(qa_copied, s + 1)
                pe.wait_ge(qkb_copied, 2 * (s + 1))
                pe.wait_ge(kd_ready, 2 * (s + 1))
                if s == 0:
                    pe.wait_ge(consts_set, 3)
                for g in range(4):
                    if g % 2 == 0 and s:
                        pe.wait_ge(dif_ready, 2 * s - 1 + g // 2)
                    for lo, hi, q, kd in ((0, HA, qa, kda), (HA, H, qb, kdb)):
                        for j in range(4):
                            b = 4 * g + j
                            col = (g % 2) * H * NT
                            last = pe.matmul(scB[g // 2][32 * j:32 * j + 32, col + lo * NT:col + hi * NT],
                                             q[:, s, b * NT:b * NT + 32], kd[:, s % 2, :, b * NT:(b + 1) * NT], start=True, stop=True)
                    if g % 2:
                        last.then_inc(pe_sc, 1)

            def turn_probs(s):
                for i in range(2):
                    pe.wait_ge(prob_ready, 2 * s + i + 1)
                    if i == 0:
                        if s:
                            pe.wait_ge(lg_copied, s)
                    elif s < ST - 1:
                        pe.wait_ge(qkb_copied, 2 * (s + 2))
                    else:
                        pe.wait_ge(pT_copied, 2 * s)
                    for g in range(4):
                        last = pe.transpose(pTB[i][0:KR, g * P:(g + 1) * P], prob[:, i, g], ident[:])
                    last.then_inc(pe_pT, 1)

            def attend(s):
                if s < ST - 1:
                    pe.wait_ge(qa_copied, s + 2)
                    pe.wait_ge(ka_copied, s + 2)
                else:
                    pe.wait_ge(oT_copied, 2 * s)
                pe.wait_ge(pT_copied, 2 * s + 2)
                pe.wait_ge(vd_ready, 2 * (s + 1))
                for c in range(2):
                    for b in range(SB):
                        g, j = b // 4, b % 4
                        last = pe.matmul(oTB[c][0:C, b * NT:(b + 1) * NT], vd[:, s % 2, c, b], pT[:, g // 2, 2 * (g % 2) + c, j],
                                         start=True, stop=True)
                    last.then_inc(pe_oT, 1)

            def project_out(s):
                pe.wait_ge(oT_copied, 2 * (s + 1))
                if s == 0:
                    pe.wait_ge(in_wout, 16)
                    pe.wait_ge(h_added, 3)
                elif s == 1:
                    pe.wait_ge(h_added, 4)
                else:
                    pe.wait_ge(h2_added, s)
                for t in range(2):
                    for c in range(2):
                        last = pe.matmul(tokB[:, t], oT[:, c, s, 8 * t:8 * t + 8].rearrange("p n b -> p (n b)"), wout[:, c], start=(c == 0), stop=(c == 1))
                last.then_inc(pe_o, 1)
                if s == ST - 1:
                    for c in range(2):
                        last = pe.matmul(bank[5][0:B, 0:D], oTc[:, c], wout[:, c], start=(c == 0), stop=(c == 1))
                    last.then_inc(pe_o, 1)

            def logits(s):
                pe.wait_ge(h2n_ready, s + 1)
                if s < ST - 1:
                    pe.wait_ge(v_copied, s + 3)
                else:
                    pe.wait_ge(h2T_copied, s)
                for c in range(2):
                    for t in range(2):
                        last = pe.transpose(trB[0:C, (2 * c + t) * P:(2 * c + t + 1) * P], h2n[:, t, c * C:(c + 1) * C], ident[:])
                last.then_inc(pe_h2T, 1)
                if s == ST - 1:
                    for c in range(2):
                        last = pe.transpose(bank[6][0:C, c * B:(c + 1) * B], h2n[0:B, 2, c * C:(c + 1) * C], ident[0:B, 0:B])
                    last.then_inc(pe_h2T, 1)
                pe.wait_ge(h2T_copied, s + 1)
                pe.wait_ge(pT_copied, 2 * s + 1)
                if s == 0:
                    pe.wait_ge(in_win, 16)
                for t in range(2):
                    for c in range(2):
                        last = pe.matmul(lgB[:, t * NODES:(t + 1) * NODES], h2T[:, c, t], win[:, c], start=(c == 0), stop=(c == 1))
                last.then_inc(pe_lg, 1)
                if s == ST - 1:
                    pe.wait_ge(h2T_copied, s + 2)
                    pe.wait_ge(lg_copied, ST)
                    pe.wait_ge(gelu_done, 2)
                    for c in range(2):
                        last = pe.matmul(lgB[0:B, 64:64 + NODES], h2T[:, c, 2, 0:B], win[:, c], start=(c == 0), stop=(c == 1))
                    last.then_inc(pe_lg, 1)

            def turn_coef(b, tiles):
                for i, t in enumerate(tiles):
                    r = rows(t)
                    last = pe.transpose(bank[b][0:NODES, i * P:i * P + r], coef[0:r, t], ident[0:r, 0:r])
                last.then_inc(pe_cT, 1)

            def tree_out(g):
                for i, t in enumerate((2 * g, 2 * g + 1) if g < ST else (TILES,)):
                    r = rows(t)
                    last = pe.matmul(finB[g][0:r, i * D:(i + 1) * D], cT[:, t, 0:r], wnode[:], start=True, stop=True)
                last.then_inc(pe_fin, 1)

            pe.wait_ge(in_ident, 16)
            pe.wait_ge(hn_ready, 1)
            for c in range(2):
                last = pe.transpose(trB[0:C, c * B:(c + 1) * B], hn[0:B, 1, 0, c * C:(c + 1) * C], ident[0:B, 0:B])
            last.then_inc(pe_hT, 1)
            project_patches(0)
            pe.wait_ge(hT_copied, 1)
            pe.wait_ge(in_wqkv, 16)
            for c in range(2):
                last = pe.matmul(bank[4][0:1, 0:D], hnT[:, c, 0, 0, 0:1], wqkv[:, c, 2 * D:3 * D], start=(c == 0), stop=(c == 1))
            last.then_inc(pe_v, 1)
            project_patches(1)
            turn_hn(0)
            qkv(0)
            project_patches(2)
            for s in range(ST):
                scores(s)
                if s:
                    logits(s - 1)
                if s < ST - 1:
                    turn_hn(s + 1)
                    qkv(s + 1)
                turn_probs(s)
                attend(s)
                project_out(s)
                if s == 0:
                    project_patches(3)
            pe.wait_ge(coef_ready, 1)
            pe.wait_ge(pT_copied, 2 * ST)
            turn_coef(4, (0, 1, 2, 3))
            pe.wait_ge(h2_added, ST + 1)
            turn_coef(5, (4, 5))
            pe.wait_ge(oT_copied, 2 * ST)
            pe.wait_ge(in_wnode, 16)
            pe.wait_ge(cT_copied, 1)
            tree_out(0)
            tree_out(1)
            pe.wait_ge(cT_copied, 2)
            tree_out(2)
            logits(ST - 1)
            pe.wait_ge(coef_ready, 3)
            turn_coef(4, (6, 7, 8))
            pe.wait_ge(cT_copied, 3)
            pe.wait_ge(fin_ready, 2)
            tree_out(3)
            tree_out(4)


def kernel(**inputs):
    import numpy as _np
    import concourse.bacc as _bacc
    from concourse import mybir as _mybir
    from concourse.bass_utils import run_bass_kernel_spmd as _run

    a = {k: _np.asarray(v) for k, v in inputs.items()}
    xt = a["x"].reshape(ST, SB, 4, 16, 4, 16, 3).transpose(3, 5, 6, 0, 2, 4, 1).reshape(KC, P, ST, SB * NP)
    xt = _np.ascontiguousarray(xt.transpose(2, 1, 0, 3))
    w_tok = a["L0_tok_W"].reshape(KC, P, D).transpose(1, 0, 2)
    pos = _np.repeat(a["L0_tok_pos_emb"], SB, 0).reshape(2, P, D)
    posb = _np.stack([pos[0], pos[1], _np.tile(a["L0_tok_b"], (P, 1))], 1)
    wq, wk, wv = _np.split(a["L0_attn_w_qkv"], 3)
    bq, bk, bv = _np.split(a["L0_attn_b_qkv"], 3)
    w = _np.concatenate([wq[:P], wk[:P], wq[P:], wk[P:], wv])
    w_qkv = w.T.reshape(2, C, 3 * D).transpose(1, 0, 2)
    last64 = [_np.concatenate([b[P:], b[P:]]) for b in (bq, bk)]
    b_qkv = _np.stack([bq[:P], bk[:P], last64[0], last64[1]], 1)
    w_out = a["L0_attn_w_out"].T.reshape(2, C, D).transpose(1, 0, 2)
    w_in = a["L0_ffn_weights_in"].T.reshape(2, C, NODES).transpose(1, 0, 2)
    masks = _np.zeros((P, HA + HC), _np.float32)
    masks[_np.arange(P), _np.arange(P) // HD] = 1.0
    masks[_np.arange(P), HA + _np.arange(P) % HC] = 1.0
    arrays = {
        "xt": xt, "w_tok": w_tok, "posb": posb, "w_qkv": w_qkv, "b_qkv": b_qkv, "w_out": w_out,
        "bv": bv.reshape(2, C).T, "bo": a["L0_attn_b_out"].reshape(1, D), "cls_tok": a["cls_tok"].reshape(1, D),
        "w_in": w_in, "w_node": a["L0_ffn_weights_out"], "masks": masks, "ident_d": _np.eye(P, dtype=_np.float32),
    }
    arrays = {k: _np.ascontiguousarray(v) for k, v in arrays.items()}
    nc = _bacc.Bacc("TRN2", target_bir_lowering=False, num_devices=1)
    f32 = _mybir.dt.float32
    args = {k: nc.dram_tensor(k, v.shape, f32, kind="ExternalInput").ap() for k, v in arrays.items()}
    out_patch = nc.dram_tensor("out_patch", (P, TILES, D), f32, kind="ExternalOutput").ap()
    out_cls = nc.dram_tensor("out_cls", (B, D), f32, kind="ExternalOutput").ap()
    vit_block(nc, out_patch=out_patch, out_cls=out_cls, **args)
    r = _run(nc, [arrays], core_ids=[0])
    patch, cls = r.results[0]["out_patch"], r.results[0]["out_cls"]
    patch = patch.reshape(8, SB, ST, 2, D).transpose(2, 1, 3, 0, 4).reshape(B, NP, D)
    return _np.concatenate([cls[:, None, :], patch], 1)
```

```python
import numpy as np
import concourse.bass as bass
from concourse import mybir
from contextlib import ExitStack

B, NP, D, PD = 64, 16, 192, 768
NT = NP + 1
H, HD = 12, 16
NODES = 21
NI = 10
LEAF = 15
FEAT = NODES + (NODES - 1 - NI) + (NODES - 1 - LEAF) + 1
P = 128
ST = 4
SB = B // ST
SC = SB * NT
KC = PD // P
C = D // 2
HC = H // 2
KR = NT * HC
QPAD = SC + 16
HA, HB = 8, 4
TILES = B * NP // P
ALLT = TILES + 1
EPS = 1e-5
SCALING = HD ** -0.5


def vit_block(nc, xt, w_tok, posb, w_qkv, b_qkv, w_out, bv, bo, cls_tok, w_in, w_node, masks, ident_d,
              out_patch, out_cls):
    fp32 = mybir.dt.float32
    ALU = mybir.AluOpType
    ACT = mybir.ActivationFunctionType
    AX = mybir.AxisListType

    v_scratch = nc.dram_tensor("v_scratch", (2, B, NP, C), fp32, kind="Internal").ap()
    vcls_scratch = nc.dram_tensor("vcls_scratch", (2, C), fp32, kind="Internal").ap()

    ctx = ExitStack()
    with ctx:
        def sb(name, shape):
            return ctx.enter_context(nc.sbuf_tensor(name, shape, fp32))

        def sem(name):
            return ctx.enter_context(nc.semaphore(name))

        wtok = sb("wtok", [P, KC, D])
        wqkv = sb("wqkv", [C, 2, 3 * D])
        wout = sb("wout", [C, 2, D])
        win = sb("win", [C, 2, NODES])
        wnode = sb("wnode", [FEAT, D])
        pos = sb("pos", [P, 3, D])
        posbias = sb("posbias", [P, 2, D])
        bqk = sb("bqk", [P, 4])
        bqs = sb("bqs", [P, 2])
        bvb = sb("bvb", [P, D])
        bob = sb("bob", [P, D])
        mask = sb("mask", [P, HA + HC])
        ident = sb("ident", [P, P])
        mhalf = sb("mhalf", [P, 3])
        x_sb = sb("x_sb", [P, ST, KC, SB * NP])
        h = sb("h", [P, ALLT, D])
        hb = sb("hb", [P, ALLT, D])
        h2 = sb("h2", [P, ALLT, D])
        fin = sb("fin", [P, ALLT, D])
        hn = sb("hn", [P, 2, 2, D])
        h2n = sb("h2n", [P, 3, D])
        stats = sb("stats", [P, 3, 6])
        mv = sb("mv", [P, ALLT, 2])
        ve = sb("ve", [P, ALLT])
        rstd = sb("rstd", [P, ALLT])
        mv2 = sb("mv2", [P, ALLT, 2])
        ve2 = sb("ve2", [P, ALLT])
        rstd2 = sb("rstd2", [P, ALLT])
        hnT = sb("hnT", [C, 2, ST, NT, SB])
        qa = sb("qa", [P, ST, QPAD])
        qb = sb("qb", [64, ST, QPAD])
        kb = sb("kb", [64, 2, SC])
        kda = sb("kda", [P, 2, HA, SC])
        kdb = sb("kdb", [64, 2, HB, SC])
        v_sb = sb("v_sb", [P, 2, 2, D])
        vcls = sb("vcls", [1, D])
        vc = sb("vc", [KR, 2, B, HD])
        vd = sb("vd", [KR, 2, 2, SB, C])
        smax = sb("smax", [P, 2, 24])
        dif = sb("dif", [P, 2, 2 * H * NT])
        ex = sb("ex", [P, 2, 4, KR])
        rsum = sb("rsum", [P, 2, 24])
        rinv = sb("rinv", [P, 2, 24])
        pT = sb("pT", [KR, 2, 4, P])
        att = sb("att", [P, 2, 2, D])
        oT = sb("oT", [C, 2, ST, NP, SB])
        oTc = sb("oTc", [C, 2, B])
        h2T = sb("h2T", [C, 2, 3, P])
        logit = sb("logit", [P, ALLT, NODES])
        gel = sb("gel", [P, ALLT, NODES])
        side = sb("side", [P, ALLT, NI, 2])
        path = sb("path", [P, ALLT, NODES])
        coef = sb("coef", [P, ALLT, FEAT])
        cT = sb("cT", [FEAT, ALLT, P])

        bank = [ctx.enter_context(nc.psum_tensor(f"bank{i}", [P, 512], fp32)) for i in range(8)]
        tokB = bank[0][:, 0:2 * D].rearrange("p (t d) -> p t d", t=2)
        embedB = [(bank[0][:, 0:D], bank[5][:, 0:D])] + [(b[:, 0:D], b[:, D:2 * D]) for b in (bank[6], bank[0], bank[7])]
        trB = bank[1]
        qaB, kaB, qkbB = bank[2], bank[3], bank[4]
        attB = [bank[2], bank[3]]
        oTB = [bank[4], bank[7]]
        scB = [bank[5], bank[6]]
        pTB = [bank[7], bank[4]]
        lgB = bank[1]
        clsoB = bank[5]
        coefB = [bank[4], bank[7], bank[4]]
        finB = [bank[2], bank[3], bank[6], bank[0], bank[5]]

        in_x = [sem(f"in_x{s}") for s in range(ST)]
        in_wtok2, in_x0b, in_wtok, in_ident, in_pos, in_cls, in_wqkv = sem("in_wtok2"), sem("in_x0b"), sem("in_wtok"), sem("in_ident"), sem("in_pos"), sem("in_cls"), sem("in_wqkv")
        in_bqk, in_mask, in_wout, in_win, in_wnode = sem("in_bqk"), sem("in_mask"), sem("in_wout"), sem("in_win"), sem("in_wnode")
        in_bv, in_bo = sem("in_bv"), sem("in_bo")
        vcls_stored, v_stored = sem("vcls_stored"), sem("v_stored")
        vcls_back = sem("vcls_back")
        v_back = [sem(f"v_back{s}") for s in range(ST)]
        out_done = sem("out_done")
        pe_h, pe_hT, pe_qa, pe_ka, pe_qkb, pe_v = sem("pe_h"), sem("pe_hT"), sem("pe_qa"), sem("pe_ka"), sem("pe_qkb"), sem("pe_v")
        pe_sc, pe_pT, pe_att, pe_oT, pe_o, pe_h2T, pe_lg = sem("pe_sc"), sem("pe_pT"), sem("pe_att"), sem("pe_oT"), sem("pe_o"), sem("pe_h2T"), sem("pe_lg")
        pe_cT, pe_fin = sem("pe_cT"), sem("pe_fin")
        hT_copied, qa_copied, qb_copied = sem("hT_copied"), sem("qa_copied"), sem("qb_copied")
        exp_done, pT_copied, oT_copied, h2T_copied, lg_copied, vcls_added, kb_copied = sem("exp_done"), sem("pT_copied"), sem("oT_copied"), sem("h2T_copied"), sem("lg_copied"), sem("vcls_added"), sem("kb_copied")
        gelu_done, cT_copied, bqs_done = sem("gelu_done"), sem("cT_copied"), sem("bqs_done")
        v_added, h_added, hn_ready, ve_ready, dif_ready, att_ready, kda_ready, sum_done = sem("v_added"), sem("h_added"), sem("hn_ready"), sem("ve_ready"), sem("dif_ready"), sem("att_ready"), sem("kda_ready"), sem("sum_done")
        h2_added, h2n_ready, ve2_ready, coef_ready, fin_ready = sem("h2_added"), sem("h2n_ready"), sem("ve2_ready"), sem("coef_ready"), sem("fin_ready")
        dve_step, sides_read = sem("dve_step"), sem("sides_read")
        consts_set, rstd_ready, rstd2_ready, kdb_ready, vd_ready, hb_ready = (
            sem("consts_set"), sem("rstd_ready"), sem("rstd2_ready"), sem("kdb_ready"), sem("vd_ready"), sem("hb_ready"))

        block = ctx.enter_context(nc.Block())

        def rows(t):
            return P if t < TILES else B

        @block.sync
        def _(sp):
            K2 = KC // 2
            sp.dma_start(wtok[:, 0:K2], w_tok[:, 0:K2]).then_inc(in_wtok, 16)
            sp.dma_start(x_sb[:, 0, 0:K2], xt[0, :, 0:K2]).then_inc(in_x[0], 16)
            sp.dma_start(wtok[:, K2:], w_tok[:, K2:]).then_inc(in_wtok2, 16)
            sp.dma_start(x_sb[:, 0, K2:], xt[0, :, K2:]).then_inc(in_x0b, 16)
            sp.dma_start(x_sb[:, 1], xt[1]).then_inc(in_x[1], 16)
            sp.dma_start(wqkv[:], w_qkv).then_inc(in_wqkv, 16)
            for s in range(2, ST):
                sp.dma_start(x_sb[:, s], xt[s]).then_inc(in_x[s], 16)
            sp.dma_start(wout[:], w_out).then_inc(in_wout, 16)
            sp.dma_start(win[:], w_in).then_inc(in_win, 16)
            sp.dma_start(wnode[:], w_node).then_inc(in_wnode, 16)
            sp.wait_ge(vcls_added, 1)
            sp.dma_start(vcls_scratch.rearrange("(a c) d -> a (c d)", a=1), vcls[:]).then_inc(vcls_stored, 16)
            sp.wait_ge(vcls_stored, 16)
            for c in range(2):
                src = vcls_scratch[c].rearrange("(h d) -> h d", d=HD).unsqueeze(1).to_broadcast([HC, B, HD])
                sp.dma_start(vc[0:HC, c], src).then_inc(vcls_back, 16)
            for s in range(ST):
                sp.wait_ge(v_added, s + 1)
                for t in range(2):
                    for c in range(2):
                        dst = v_scratch[c, s * SB:(s + 1) * SB, 8 * t:8 * t + 8].rearrange("b n d -> n b d")
                        sp.dma_start(dst, v_sb[:, s % 2, t, c * C:(c + 1) * C]).then_inc(v_stored, 16)
                sp.wait_ge(v_stored, 64 * (s + 1))
                for c in range(2):
                    src = v_scratch[c, s * SB:(s + 1) * SB].rearrange("b n (h d) -> (n h) b d", d=HD)
                    sp.dma_start(vc[HC:KR, c, s * SB:(s + 1) * SB], src).then_inc(v_back[s], 16)
            stores = 0
            for g in range(ST):
                sp.wait_ge(fin_ready, g + 1)
                sp.dma_start(out_patch[:, 2 * g:2 * g + 2], fin[:, 2 * g:2 * g + 2]).then_inc(out_done, 16)
                stores += 16
            sp.wait_ge(fin_ready, ST + 1)
            sp.dma_start(out_cls, fin[0:B, TILES]).then_inc(out_done, 16)
            sp.wait_ge(out_done, stores + 16)

        @block.gpsimd
        def _(pool):
            pool.memset(mhalf[:], -0.5).then_inc(consts_set, 1)
            pool.memset(qa[:, :, SC:], 0.0).then_inc(consts_set, 1)
            pool.memset(qb[:, :, SC:], 0.0).then_inc(consts_set, 1)
            pool.memset(h2T[:, :, 2, B:], 0.0).then_inc(consts_set, 1)
            pool.memset(coef[:, :, 0:1], 0.0).then_inc(consts_set, 1)

            def root(n, t0, nt, r):
                pool.wait_ge(ve_ready, n + 1)
                pool.tensor_tensor(rstd[0:r, t0:t0 + nt], ve[0:r, t0:t0 + nt], mhalf[0:r, 0:nt], ALU.pow).then_inc(rstd_ready, 1)

            def root2(s):
                pool.wait_ge(ve2_ready, s + 1)
                nt = 2 if s < ST - 1 else 3
                pool.tensor_tensor(rstd2[:, 2 * s:2 * s + nt], ve2[:, 2 * s:2 * s + nt], mhalf[:, 0:nt], ALU.pow).then_inc(rstd2_ready, 1)

            def add_bias_out(s):
                pool.wait_ge(h_added, s + 1)
                pool.tensor_tensor(hb[:, 2 * s:2 * s + 2], h[:, 2 * s:2 * s + 2], bob[:].unsqueeze(1).to_broadcast([P, 2, D]), ALU.add).then_inc(hb_ready, 1)

            def spread_keys(s):
                pool.wait_ge(kb_copied, s + 1)
                if s >= 2:
                    pool.wait_ge(pe_sc, 2 * (s - 1))
                pool.tensor_tensor(kdb[:, s % 2], kb[:, s % 2].unsqueeze(1).to_broadcast([64, HB, SC]),
                                   mask[0:64, 0:HB].unsqueeze(2).to_broadcast([64, HB, SC]), ALU.mult).then_inc(kdb_ready, 1)

            def spread_values(s):
                if s == 0:
                    pool.wait_ge(vcls_back, 32)
                pool.wait_ge(v_back[s], 32)
                if s >= 2:
                    pool.wait_ge(pe_att, 2 * (s - 1))
                for c in range(2):
                    pool.tensor_tensor(vd[:, s % 2, c].rearrange("p b (h d) -> p b h d", d=HD),
                                       vc[:, c, s * SB:(s + 1) * SB].unsqueeze(2).to_broadcast([KR, SB, HC, HD]),
                                       mask[0:KR, HA:HA + HC].unsqueeze(1).unsqueeze(3).to_broadcast([KR, SB, HC, HD]),
                                       ALU.mult).then_inc(vd_ready, 1)

            pool.wait_ge(consts_set, 6)
            root(0, TILES, 1, B)
            root(1, 0, 2, P)
            pool.wait_ge(in_bo, 16)
            pool.wait_ge(in_cls, 16)
            pool.tensor_tensor(hb[0:B, TILES], h[0:B, TILES], bob[0:B], ALU.add).then_inc(hb_ready, 1)
            root(2, 2, 2, P)
            add_bias_out(0)
            root(3, 4, 2, P)
            pool.wait_ge(in_mask, 16)
            spread_keys(0)
            root(4, 6, 2, P)
            spread_values(0)
            spread_keys(1)
            add_bias_out(1)
            for s in range(ST):
                if s < ST - 1:
                    spread_values(s + 1)
                root2(s)
                if s < 2:
                    spread_keys(s + 2)
                    add_bias_out(s + 2)

        @block.scalar
        def _(sc):
            sc.dma_start(h[0:B, TILES], cls_tok.to_broadcast([B, D])).then_inc(in_cls, 16)
            sc.dma_start(ident[:], ident_d).then_inc(in_ident, 16)
            sc.dma_start(bqk[:], b_qkv).then_inc(in_bqk, 16)
            sc.dma_start(pos[:], posb).then_inc(in_pos, 16)
            sc.dma_start(mask[:], masks).then_inc(in_mask, 16)
            sc.dma_start(bvb[:], bv.to_broadcast([P, D])).then_inc(in_bv, 16)
            sc.dma_start(bob[:], bo.to_broadcast([P, D])).then_inc(in_bo, 16)

            def copy_hT(s):
                sc.wait_ge(pe_hT, s + 2)
                if s >= 0:
                    src = trB[0:C, :].rearrange("p (c n b) -> p c n b", c=2, n=NP)
                    sc.activation(hnT[:, :, s, 1:NT], src, ACT.Copy).then_inc(hT_copied, 1)
                else:
                    sc.activation(hnT[:, :, :, 0], trB[0:C, 0:2 * B].rearrange("p (c s b) -> p c s b", c=2, s=ST), ACT.Copy).then_inc(hT_copied, 1)

            def by_image(ap):
                return ap.rearrange("p (n b) -> p b n", b=SB)

            def copy_qk(s):
                if s == 0:
                    sc.wait_ge(bqs_done, 1)
                sc.wait_ge(pe_qkb, s + 1)
                sc.activation(qb[:, s, 0:SC].rearrange("p (b n) -> p b n", n=NT), by_image(qkbB[0:64, 0:SC]), ACT.Identity,
                              bias=bqs[0:64, 1:2], scale=SCALING).then_inc(qb_copied, 1)
                if s >= 2:
                    sc.wait_ge(kdb_ready, s - 1)
                sc.activation(kb[:, s % 2].rearrange("p (b n) -> p b n", n=NT), by_image(qkbB[64:P, 0:SC]), ACT.Identity,
                              bias=bqk[0:64, 3:4]).then_inc(kb_copied, 1)
                sc.wait_ge(pe_qa, s + 1)
                sc.activation(qa[:, s, 0:SC].rearrange("p (b n) -> p b n", n=NT), by_image(qaB[:, 0:SC]), ACT.Identity,
                              bias=bqs[:, 0:1], scale=SCALING).then_inc(qa_copied, 1)

            def exps(s, i):
                sc.wait_ge(dif_ready, 2 * s + i + 1)
                if s:
                    sc.wait_ge(sum_done, 2 * (s - 1) + i + 1)
                    sc.wait_ge(pe_pT, 2 * (s - 1) + i + 1)
                sc.activation(ex[:, i].rearrange("p g (k h) -> p g h k", h=HC),
                              dif[:, i].rearrange("p (g h k) -> p g h k", g=4, k=NT), ACT.Exp, bias=mone).then_inc(exp_done, 1)

            def copy_pT(s, i):
                sc.wait_ge(pe_pT, 2 * s + i + 1)
                if s:
                    sc.wait_ge(pe_att, 2 * (s - 1) + i + 1)
                sc.activation(pT[:, i], pTB[i][0:KR, :].rearrange("p (g q) -> p g q", g=4), ACT.Copy).then_inc(pT_copied, 1)

            def copy_oT(s):
                for i in range(2):
                    sc.wait_ge(pe_oT, 2 * s + 1 + i)
                    src = oTB[i][0:C, :].rearrange("p (c b q) -> p c b q", c=2, q=32)
                    sc.activation(oT[:, :, s, :, 8 * i:8 * i + 8].rearrange("p c n b -> p c b n"), src[:, :, :, 1:NT], ACT.Copy)
                    sc.activation(oTc[:, :, s * SB + 8 * i:s * SB + 8 * i + 8], src[:, :, :, 0], ACT.Copy).then_inc(oT_copied, 1)

            def copy_h2T(s):
                sc.wait_ge(pe_h2T, s + 1)
                if s:
                    sc.wait_ge(pe_lg, s)
                sc.activation(h2T[:, :, 0:2], trB[0:C, :].rearrange("p (c t q) -> p c t q", c=2, q=P), ACT.Copy).then_inc(h2T_copied, 1)

            def copy_logits(s):
                sc.wait_ge(pe_lg, s + 1)
                sc.wait_ge(rstd2_ready, s + 1)
                for t in range(2):
                    last = sc.activation(logit[:, 2 * s + t], lgB[:, t * NODES:(t + 1) * NODES], ACT.Copy, scale=rstd2[:, 2 * s + t:2 * s + t + 1])
                last.then_inc(lg_copied, 1)

            mone = -1.0
            sc.wait_ge(in_bqk, 16)
            sc.activation(bqs[:], bqk[:].rearrange("p (a b) -> p b a", b=2)[:, 0], ACT.Copy, scale=SCALING).then_inc(bqs_done, 1)
            copy_hT(-1)
            copy_hT(0)
            copy_qk(0)
            copy_hT(1)
            exps(0, 0)
            exps(0, 1)
            copy_qk(1)
            for s in range(ST):
                if s == ST - 2:
                    copy_pT(s, 0)
                    copy_pT(s, 1)
                    copy_h2T(s - 1)
                    copy_logits(s - 1)
                    exps(s + 1, 0)
                    exps(s + 1, 1)
                    copy_oT(s)
                    continue
                copy_pT(s, 0)
                copy_pT(s, 1)
                if s:
                    copy_h2T(s - 1)
                    copy_logits(s - 1)
                if s < ST - 2:
                    exps(s + 1, 0)
                copy_oT(s)
                if s < ST - 2:
                    copy_hT(s + 2)
                    exps(s + 1, 1)
                    copy_qk(s + 2)
            sc.wait_ge(lg_copied, ST - 1)
            sc.activation(gel[:, 0:6], logit[:, 0:6], ACT.Gelu).then_inc(gelu_done, 1)
            for i, (t0, nt) in enumerate(((0, 4), (4, 2))):
                sc.wait_ge(pe_cT, i + 1)
                sc.activation(cT[:, t0:t0 + nt], coefB[i][0:FEAT, 0:nt * P].rearrange("p (t q) -> p t q", q=P), ACT.Copy).then_inc(cT_copied, 1)
            copy_h2T(ST - 1)
            sc.wait_ge(pe_h2T, ST + 1)
            sc.activation(h2T[:, :, 2, 0:B], bank[7][0:C, 0:2 * B].rearrange("p (c q) -> p c q", c=2), ACT.Copy).then_inc(h2T_copied, 1)
            sc.wait_ge(sides_read, 1)
            sc.wait_ge(rstd2_ready, ST)
            for t in range(6, ALLT):
                last = sc.activation(gel[:, t], lgB[:, (t - 6) * NODES:(t - 5) * NODES], ACT.Gelu, scale=rstd2[:, t:t + 1])
            last.then_inc(gelu_done, 1)
            sc.wait_ge(pe_cT, 3)
            sc.activation(cT[:, 6:9], coefB[2][0:FEAT, 0:3 * P].rearrange("p (t q) -> p t q", q=P), ACT.Copy).then_inc(cT_copied, 1)

        @block.vector
        def _(dve):
            steps = [0]

            def after(ins):
                steps[0] += 1
                ins.then_inc(dve_step, 1)
                dve.wait_ge(dve_step, steps[0])

            def moments(src, tiles, mv_, ve_, ve_sem):
                for i, t in enumerate(tiles):
                    r = rows(t)
                    last = dve.bn_stats(stats[0:r, i], src[0:r, t])
                after(last)
                for i, t in enumerate(tiles):
                    last = dve.bn_aggr(mv_[0:rows(t), t], stats[0:rows(t), i])
                after(last)
                rr = P if len(tiles) > 1 else rows(tiles[0])
                T = slice(tiles[0], tiles[-1] + 1)
                dve.tensor_scalar(ve_[0:rr, T], mv_[0:rr, T, 1], EPS, None, ALU.add).then_inc(ve_sem, 1)

            def layernorm1(tiles, rstd_at, dst):
                moments(h, tiles, mv, ve, ve_ready)
                dve.wait_ge(rstd_ready, rstd_at)
                for i, t in enumerate(tiles):
                    r = rows(t)
                    last = dve.tensor_scalar(dst[0:r, i], h[0:r, t], mv[0:r, t, 0:1], rstd[0:r, t:t + 1], ALU.subtract, ALU.mult)
                last.then_inc(hn_ready, 1)

            def embed(s):
                dve.wait_ge(pe_h, s + 1)
                if s == 0:
                    dve.tensor_tensor(h[:, 0], embedB[0][0], posbias[:, 0], ALU.add)
                    dve.tensor_tensor(h[:, 1], embedB[0][1], posbias[:, 1], ALU.add).then_inc(h_added, 1)
                else:
                    bk = (None, bank[6], bank[0], bank[7])[s]
                    dve.tensor_tensor(h[:, 2 * s:2 * s + 2], bk[:, 0:2 * D].rearrange("p (t d) -> p t d", t=2), posbias[:], ALU.add).then_inc(h_added, 1)
                dve.wait_ge(h_added, s + 1)
                if s >= 2:
                    dve.wait_ge(pe_hT, s)
                layernorm1((2 * s, 2 * s + 1), s + 2, hn[:, s % 2])

            def spread_keys(s):
                dve.wait_ge(pe_ka, s + 1)
                if s == 0:
                    dve.wait_ge(in_mask, 16)
                    dve.wait_ge(in_bqk, 16)
                if s >= 2:
                    dve.wait_ge(pe_sc, 2 * (s - 1))
                for hs in (0, HA // 2):
                    full = [P, HA // 2, SC]
                    dve.scalar_tensor_tensor(out=kda[:, s % 2, hs:hs + HA // 2],
                                             in0=kaB[:, 0:SC].unsqueeze(1).to_broadcast(full),
                                             scalar=bqk[:, 1:2],
                                             in1=mask[:, hs:hs + HA // 2].unsqueeze(2).to_broadcast(full),
                                             op0=ALU.add, op1=ALU.mult).then_inc(kda_ready, 1)

            def add_value_bias(s):
                dve.wait_ge(pe_v, s + 2)
                if s >= 2:
                    dve.wait_ge(v_stored, 64 * (s - 1))
                dve.tensor_tensor(v_sb[:, s % 2], trB[:, 0:2 * D].rearrange("p (t d) -> p t d", t=2),
                                  bvb[:].unsqueeze(1).to_broadcast([P, 2, D]), ALU.add).then_inc(v_added, 1)

            def shift_scores(s):
                for i in range(2):
                    dve.wait_ge(pe_sc, 2 * s + i + 1)
                    scores = scB[i][:, 0:2 * H * NT].rearrange("p (h k) -> p h k", k=NT)
                    after(dve.tensor_reduce(out=smax[:, i], in_=scores, axis=AX.X, op=ALU.max))
                    if s:
                        dve.wait_ge(exp_done, 2 * s + i - 1)
                    dve.scalar_tensor_tensor(out=dif[:, i].rearrange("p (h k) -> p h k", k=NT), in0=scores, scalar=1.0,
                                             in1=smax[:, i].unsqueeze(2).to_broadcast([P, 2 * H, NT]),
                                             op0=ALU.add, op1=ALU.subtract).then_inc(dif_ready, 1)

            def row_sums(s):
                for i in range(2):
                    dve.wait_ge(exp_done, 2 * s + i + 1)
                    dve.tensor_reduce(out=rsum[:, i], in_=ex[:, i].rearrange("p g (k h) -> p g h k", h=HC), axis=AX.X,
                                      op=ALU.add).then_inc(sum_done, 1)
                dve.wait_ge(sum_done, 2 * s + 2)
                after(dve.reciprocal(rinv[:], rsum[:]))

            def normalise(s):
                for i in range(2):
                    dve.wait_ge(pe_att, 2 * s + i + 1)
                    if s:
                        dve.wait_ge(pe_oT, 2 * (s - 1) + i + 1)
                    dve.tensor_tensor(att[:, i].rearrange("p g (h d) -> p (g h) d", d=HD),
                                      attB[i][:, 0:2 * D].rearrange("p (h d) -> p h d", d=HD),
                                      rinv[:, i].unsqueeze(2).to_broadcast([P, 2 * H, HD]), ALU.mult).then_inc(att_ready, 1)

            def residual(s):
                dve.wait_ge(pe_o, s + 1)
                dve.wait_ge(hb_ready, s + 2)
                dve.tensor_tensor(h2[:, 2 * s:2 * s + 2], tokB, hb[:, 2 * s:2 * s + 2], ALU.add).then_inc(h2_added, 1)
                if s == ST - 1:
                    dve.wait_ge(pe_o, s + 2)
                    dve.tensor_tensor(h2[0:B, TILES], clsoB[0:B, 0:D], hb[0:B, TILES], ALU.add).then_inc(h2_added, 1)
                    dve.wait_ge(h2_added, s + 2)
                else:
                    dve.wait_ge(h2_added, s + 1)
                if s:
                    dve.wait_ge(pe_h2T, s)
                tiles = (2 * s, 2 * s + 1) if s < ST - 1 else (2 * s, 2 * s + 1, TILES)
                moments(h2, tiles, mv2, ve2, ve2_ready)
                for i, t in enumerate(tiles):
                    r = rows(t)
                    last = dve.tensor_scalar(h2n[0:r, i], h2[0:r, t], mv2[0:r, t, 0:1], None, ALU.subtract)
                last.then_inc(h2n_ready, 1)

            def tree(t0, nt, src, gelus):
                T = slice(t0, t0 + nt)
                dve.tensor_scalar(side[:, T, :, 0], src, 0.0, None, ALU.is_le)
                last = dve.tensor_scalar(side[:, T, :, 1], src, 0.0, None, ALU.is_gt)
                if nt == 3:
                    last.then_inc(sides_read, 1)
                    dve.wait_ge(sides_read, 1)
                else:
                    after(last)
                dve.tensor_copy(path[:, T, 1:3], side[:, T, 0])

                def down(parents, a, n):
                    return dve.tensor_tensor(path[:, T, 2 * a + 1:2 * (a + n) + 1].rearrange("p t (n e) -> p t n e", e=2),
                                             parents.unsqueeze(3).to_broadcast([P, nt, n, 2]),
                                             side[:, T, a:a + n], ALU.mult)
                after(down(side[:, T, 0], 1, 2))
                after(down(path[:, T, 3:7], 3, 4))
                after(down(path[:, T, 7:NI], 7, NI - 7))
                dve.wait_ge(gelu_done, gelus)
                dve.tensor_tensor(coef[:, T, 1:NODES].rearrange("p t (n e) -> p t n e", e=2),
                                  gel[:, T, 0:NI].unsqueeze(3).to_broadcast([P, nt, NI, 2]),
                                  path[:, T, 1:NODES].rearrange("p t (n e) -> p t n e", e=2), ALU.mult)
                own = NODES + NODES - 1 - NI
                last20 = gel[:, T, NODES - 1:NODES]
                dve.tensor_tensor(coef[:, T, NODES:own], path[:, T, NI:NODES - 1], gel[:, T, NI:NODES - 1], ALU.mult)
                dve.tensor_scalar(coef[:, T, own:own + 1], last20, 6.0, None, ALU.mult)
                dve.scalar_tensor_tensor(out=coef[:, T, own + 1:FEAT], in0=path[:, T, LEAF:NODES - 1], scalar=-1.0,
                                         in1=last20.to_broadcast([P, nt, NODES - 1 - LEAF]), op0=ALU.mult, op1=ALU.mult).then_inc(coef_ready, 1)

            dve.memset(mv2[B:P, TILES], 1.0).then_inc(consts_set, 1)
            dve.wait_ge(consts_set, 6)
            dve.wait_ge(in_cls, 16)
            layernorm1((TILES,), 1, hn[:, 1])
            dve.wait_ge(in_pos, 16)
            after(dve.tensor_tensor(posbias[:], pos[:, 0:2], pos[:, 2:3].to_broadcast([P, 2, D]), ALU.add))
            embed(0)
            dve.wait_ge(pe_v, 1)
            dve.wait_ge(in_bv, 16)
            dve.tensor_tensor(vcls[:], bank[4][0:1, 0:D], bvb[0:1], ALU.add).then_inc(vcls_added, 1)
            dve.wait_ge(pe_hT, 1)
            embed(1)
            add_value_bias(0)
            spread_keys(0)
            embed(2)
            embed(3)
            shift_scores(0)
            add_value_bias(1)
            spread_keys(1)
            row_sums(0)
            for s in range(ST):
                if s == ST - 2:
                    shift_scores(s + 1)
                    normalise(s)
                    row_sums(s + 1)
                    residual(s)
                else:
                    normalise(s)
                    if s < ST - 2:
                        shift_scores(s + 1)
                        residual(s)
                        add_value_bias(s + 2)
                        spread_keys(s + 2)
                        row_sums(s + 1)
            dve.wait_ge(lg_copied, ST - 1)
            tree(0, 6, logit[:, 0:6, 0:NI], 1)
            residual(ST - 1)

            def finish(g):
                dve.wait_ge(pe_fin, g + 1)
                if g < ST:
                    dve.tensor_tensor(fin[:, 2 * g:2 * g + 2], finB[g][:, 0:2 * D].rearrange("p (t d) -> p t d", t=2),
                                      h2[:, 2 * g:2 * g + 2], ALU.add).then_inc(fin_ready, 1)
                else:
                    dve.tensor_tensor(fin[0:B, TILES], finB[g][0:B, 0:D], h2[0:B, TILES], ALU.add).then_inc(fin_ready, 1)
            for g in range(3):
                finish(g)
            dve.wait_ge(pe_lg, ST)
            tree(6, 3, lgB[:, 0:3 * NODES].rearrange("p (t n) -> p t n", n=NODES)[:, :, 0:NI], 2)
            finish(3)
            finish(4)

        @block.tensor
        def _(pe):
            def project_patches(s):
                pe.wait_ge(in_x[s], 16)
                if s == 0:
                    pe.wait_ge(in_wtok, 16)
                elif s == 2:
                    pe.wait_ge(h_added, 1)
                if s == 0:
                    for k in range(KC):
                        if k == KC // 2:
                            pe.wait_ge(in_wtok2, 16)
                            pe.wait_ge(in_x0b, 16)
                        for t in range(2):
                            last = pe.matmul(embedB[s][t], x_sb[:, s, k, t * P:(t + 1) * P], wtok[:, k], start=(k == 0), stop=(k == KC - 1))
                else:
                    for t in range(2):
                        for k in range(KC):
                            last = pe.matmul(embedB[s][t], x_sb[:, s, k, t * P:(t + 1) * P], wtok[:, k], start=(k == 0), stop=(k == KC - 1))
                last.then_inc(pe_h, 1)

            def turn_hn(s):
                pe.wait_ge(hn_ready, s + 2)
                if s == 0:
                    pe.wait_ge(hT_copied, 1)
                elif s < 3:
                    pe.wait_ge(v_added, s)
                else:
                    pe.wait_ge(lg_copied, 1)
                for c in range(2):
                    for t in range(2):
                        last = pe.transpose(trB[0:C, (2 * c + t) * P:(2 * c + t + 1) * P], hn[:, s % 2, t, c * C:(c + 1) * C], ident[:])
                last.then_inc(pe_hT, 1)

            def qkv(s):
                pe.wait_ge(hT_copied, s + 2)
                if s == 0:
                    pe.wait_ge(in_wqkv, 16)
                for t in range(2):
                    for c in range(2):
                        last = pe.matmul(trB[:, t * D:(t + 1) * D], hnT[:, c, s, 1 + 8 * t:9 + 8 * t].rearrange("p n b -> p (n b)"), wqkv[:, c, 2 * D:3 * D],
                                         start=(c == 0), stop=(c == 1))
                last.then_inc(pe_v, 1)
                for dst, col, done in ((kaB, 1, pe_ka), (qkbB, 2, pe_qkb), (qaB, 0, pe_qa)):
                    if dst is qkbB:
                        if s == 0:
                            pe.wait_ge(vcls_added, 1)
                        elif s == 1:
                            pe.wait_ge(kb_copied, 1)
                        else:
                            pe.wait_ge(oT_copied, 2 * (s - 1) - 1)
                    elif s == 1:
                        pe.wait_ge(qa_copied, 1) if dst is qaB else pe.wait_ge(kda_ready, 2)
                    elif s:
                        pe.wait_ge(att_ready, 2 * (s - 1))
                    for c in range(2):
                        last = pe.matmul(dst[:, 0:SC], wqkv[:, c, col * P:(col + 1) * P],
                                         hnT[:, c, s].rearrange("p n b -> p (n b)"), start=(c == 0), stop=(c == 1))
                    last.then_inc(done, 1)

            def scores(s):
                pe.wait_ge(qa_copied, s + 1)
                pe.wait_ge(qb_copied, s + 1)
                pe.wait_ge(kda_ready, 2 * (s + 1))
                pe.wait_ge(kdb_ready, s + 1)
                if s == 0:
                    pe.wait_ge(consts_set, 6)
                    pe.wait_ge(h_added, 2)
                for g in range(4):
                    if g % 2 == 0 and s:
                        pe.wait_ge(dif_ready, 2 * s - 1 + g // 2)
                    by_image = kda[:, s % 2].rearrange("p h (n b) -> p h b n", b=SB), kdb[:, s % 2].rearrange("p h (b n) -> p h b n", n=NT)
                    for lo, hi, q, kd in ((0, HA, qa, by_image[0]), (HA, H, qb, by_image[1])):
                        for j in range(4):
                            b = 4 * g + j
                            col = (g % 2) * H * NT
                            last = pe.matmul(scB[g // 2][32 * j:32 * j + 32, col + lo * NT:col + hi * NT],
                                             q[:, s, b * NT:b * NT + 32], kd[:, :, b], start=True, stop=True)
                    if g % 2:
                        last.then_inc(pe_sc, 1)

            def turn_probs(s):
                for i in range(2):
                    pe.wait_ge(exp_done, 2 * s + i + 1)
                    if i == 0 and s:
                        pe.wait_ge(oT_copied, 2 * s)
                    elif i == 0:
                        pe.wait_ge(h_added, 4)
                    if i == 1:
                        if s < ST - 1:
                            pe.wait_ge(qb_copied, s + 2)
                            pe.wait_ge(kb_copied, s + 2)
                        else:
                            pe.wait_ge(oT_copied, 2 * s - 1)
                    for g in range(4):
                        last = pe.transpose(pTB[i][0:KR, g * P:(g + 1) * P], ex[:, i, g], ident[:])
                    last.then_inc(pe_pT, 1)

            def attend(s):
                if s < ST - 1:
                    pe.wait_ge(qa_copied, s + 2)
                    pe.wait_ge(kda_ready, 2 * (s + 2))
                else:
                    pe.wait_ge(att_ready, 2 * s)
                pe.wait_ge(vd_ready, 2 * (s + 1))
                for i in range(2):
                    pe.wait_ge(pT_copied, 2 * s + i + 1)
                    for g in range(2):
                        for c in range(2):
                            for j in range(4):
                                last = pe.matmul(attB[i][32 * j:32 * j + 32, (2 * g + c) * C:(2 * g + c + 1) * C],
                                                 pT[:, i, 2 * g + c, 32 * j:32 * j + 32], vd[:, s % 2, c, 8 * i + 4 * g + j],
                                                 start=True, stop=True)
                    last.then_inc(pe_att, 1)

            def turn_outputs(s):
                for i in range(2):
                    pe.wait_ge(att_ready, 2 * s + i + 1)
                    pe.wait_ge(pT_copied, 2 * s + 2)
                    for c in range(2):
                        for g in range(2):
                            last = pe.transpose(oTB[i][0:C, (2 * c + g) * P:(2 * c + g + 1) * P], att[:, i, g, c * C:(c + 1) * C], ident[:])
                    last.then_inc(pe_oT, 1)

            def project_out(s):
                pe.wait_ge(oT_copied, 2 * (s + 1))
                if s == 0:
                    pe.wait_ge(in_wout, 16)
                    pe.wait_ge(h_added, 3)
                else:
                    pe.wait_ge(h2_added, s)
                for t in range(2):
                    for c in range(2):
                        last = pe.matmul(tokB[:, t], oT[:, c, s, 8 * t:8 * t + 8].rearrange("p n b -> p (n b)"), wout[:, c], start=(c == 0), stop=(c == 1))
                last.then_inc(pe_o, 1)
                if s == ST - 1:
                    for c in range(2):
                        last = pe.matmul(clsoB[0:B, 0:D], oTc[:, c], wout[:, c], start=(c == 0), stop=(c == 1))
                    last.then_inc(pe_o, 1)

            def turn_h2n(s):
                pe.wait_ge(h2n_ready, s + 1)
                if s < 2:
                    pe.wait_ge(v_added, s + 3)
                else:
                    pe.wait_ge(lg_copied, s)
                for c in range(2):
                    for t in range(2):
                        last = pe.transpose(trB[0:C, (2 * c + t) * P:(2 * c + t + 1) * P], h2n[:, t, c * C:(c + 1) * C], ident[:])
                last.then_inc(pe_h2T, 1)
                if s == ST - 1:
                    pe.wait_ge(cT_copied, 2)
                    for c in range(2):
                        last = pe.transpose(bank[7][0:C, c * B:(c + 1) * B], h2n[0:B, 2, c * C:(c + 1) * C], ident[0:B, 0:B])
                    last.then_inc(pe_h2T, 1)

            def logits(s):
                pe.wait_ge(h2T_copied, s + 1)
                if s == 0:
                    pe.wait_ge(in_win, 16)
                for t in range(2):
                    for c in range(2):
                        last = pe.matmul(lgB[:, t * NODES:(t + 1) * NODES], h2T[:, c, t], win[:, c], start=(c == 0), stop=(c == 1))
                if s == ST - 1:
                    pe.wait_ge(h2T_copied, s + 2)
                    for c in range(2):
                        last = pe.matmul(lgB[:, 2 * NODES:3 * NODES], h2T[:, c, 2], win[:, c], start=(c == 0), stop=(c == 1))
                last.then_inc(pe_lg, 1)

            def turn_coef(b, tiles):
                for i, t in enumerate(tiles):
                    r = rows(t)
                    last = pe.transpose(coefB[b][0:FEAT, i * P:i * P + r], coef[0:r, t], ident[0:r, 0:r])
                last.then_inc(pe_cT, 1)

            def tree_out(g):
                for i, t in enumerate((2 * g, 2 * g + 1) if g < ST else (TILES,)):
                    r = rows(t)
                    last = pe.matmul(finB[g][0:r, i * D:(i + 1) * D], cT[:, t, 0:r], wnode[:], start=True, stop=True)
                last.then_inc(pe_fin, 1)

            project_patches(0)
            pe.wait_ge(in_ident, 16)
            pe.wait_ge(hn_ready, 1)
            for c in range(2):
                last = pe.transpose(trB[0:C, c * B:(c + 1) * B], hn[0:B, 1, 0, c * C:(c + 1) * C], ident[0:B, 0:B])
            last.then_inc(pe_hT, 1)
            project_patches(1)
            pe.wait_ge(hT_copied, 1)
            pe.wait_ge(in_wqkv, 16)
            for c in range(2):
                last = pe.matmul(bank[4][0:1, 0:D], hnT[:, c, 0, 0, 0:1], wqkv[:, c, 2 * D:3 * D], start=(c == 0), stop=(c == 1))
            last.then_inc(pe_v, 1)
            turn_hn(0)
            project_patches(2)
            qkv(0)
            turn_hn(1)
            project_patches(3)
            scores(0)
            qkv(1)
            for s in range(ST):
                turn_probs(s)
                if s == ST - 2:
                    turn_h2n(s - 1)
                    scores(s + 1)
                    attend(s)
                    logits(s - 1)
                    turn_outputs(s)
                elif s == ST - 1:
                    project_out(s - 1)
                    attend(s)
                    turn_h2n(s - 1)
                    turn_outputs(s)
                    logits(s - 1)
                    project_out(s)
                else:
                    if s:
                        turn_h2n(s - 1)
                    attend(s)
                    if s:
                        logits(s - 1)
                    scores(s + 1)
                    turn_outputs(s)
                    turn_hn(s + 2)
                    project_out(s)
                    qkv(s + 2)
            pe.wait_ge(coef_ready, 1)
            turn_coef(0, (0, 1, 2, 3))
            turn_coef(1, (4, 5))
            pe.wait_ge(in_wnode, 16)
            pe.wait_ge(cT_copied, 1)
            tree_out(0)
            turn_h2n(ST - 1)
            tree_out(1)
            logits(ST - 1)
            pe.wait_ge(cT_copied, 2)
            tree_out(2)
            pe.wait_ge(coef_ready, 2)
            turn_coef(2, (6, 7, 8))
            pe.wait_ge(cT_copied, 3)
            pe.wait_ge(h2_added, ST + 1)
            tree_out(3)
            tree_out(4)


def kernel(**inputs):
    import numpy as _np
    import concourse.bacc as _bacc
    from concourse import mybir as _mybir
    from concourse.bass_utils import run_bass_kernel_spmd as _run

    a = {k: _np.asarray(v) for k, v in inputs.items()}
    xt = a["x"].reshape(ST, SB, 4, 16, 4, 16, 3).transpose(3, 5, 6, 0, 2, 4, 1).reshape(KC, P, ST, SB * NP)
    xt = _np.ascontiguousarray(xt.transpose(2, 1, 0, 3))
    w_tok = a["L0_tok_W"].reshape(KC, P, D).transpose(1, 0, 2)
    pos = _np.repeat(a["L0_tok_pos_emb"], SB, 0).reshape(2, P, D)
    posb = _np.stack([pos[0], pos[1], _np.tile(a["L0_tok_b"], (P, 1))], 1)
    wq, wk, wv = _np.split(a["L0_attn_w_qkv"], 3)
    bq, bk, bv = _np.split(a["L0_attn_b_qkv"], 3)
    w = _np.concatenate([wq[:P], wk[:P], wq[P:], wk[P:], wv])
    w_qkv = w.T.reshape(2, C, 3 * D).transpose(1, 0, 2)
    last64 = [_np.concatenate([b[P:], b[P:]]) for b in (bq, bk)]
    b_qkv = _np.stack([bq[:P], bk[:P], last64[0], last64[1]], 1)
    w_out = a["L0_attn_w_out"].T.reshape(2, C, D).transpose(1, 0, 2)
    w_in = a["L0_ffn_weights_in"].T.reshape(2, C, NODES).transpose(1, 0, 2)
    w_node = a["L0_ffn_weights_out"][_np.minimum(_np.arange(FEAT), NODES - 1)]
    masks = _np.zeros((P, HA + HC), _np.float32)
    masks[_np.arange(P), _np.arange(P) // HD] = 1.0
    masks[_np.arange(P), HA + _np.arange(P) % HC] = 1.0
    arrays = {
        "xt": xt, "w_tok": w_tok, "posb": posb, "w_qkv": w_qkv, "b_qkv": b_qkv, "w_out": w_out,
        "bv": bv.reshape(1, D), "bo": a["L0_attn_b_out"].reshape(1, D), "cls_tok": a["cls_tok"].reshape(1, D),
        "w_in": w_in, "w_node": w_node, "masks": masks, "ident_d": _np.eye(P, dtype=_np.float32),
    }
    arrays = {k: _np.ascontiguousarray(v) for k, v in arrays.items()}
    nc = _bacc.Bacc("TRN2", target_bir_lowering=False, num_devices=1)
    f32 = _mybir.dt.float32
    args = {k: nc.dram_tensor(k, v.shape, f32, kind="ExternalInput").ap() for k, v in arrays.items()}
    out_patch = nc.dram_tensor("out_patch", (P, TILES, D), f32, kind="ExternalOutput").ap()
    out_cls = nc.dram_tensor("out_cls", (B, D), f32, kind="ExternalOutput").ap()
    vit_block(nc, out_patch=out_patch, out_cls=out_cls, **args)
    r = _run(nc, [arrays], core_ids=[0])
    patch, cls = r.results[0]["out_patch"], r.results[0]["out_cls"]
    patch = patch.reshape(8, SB, ST, 2, D).transpose(2, 1, 3, 0, 4).reshape(B, NP, D)
    return _np.concatenate([cls[:, None, :], patch], 1)
```

```python
import numpy as np
import concourse.bass as bass
from concourse import mybir
from contextlib import ExitStack

B, NP, D, PD = 64, 16, 192, 768
NT = NP + 1
H, HD = 12, 16
NODES = 21
NI = 10
LEAF = 15
FEAT = NODES + (NODES - 1 - NI) + (NODES - 1 - LEAF) + 1
P = 128
ST = 4
SB = B // ST
SC = SB * NT
KC = PD // P
C = D // 2
HC = H // 2
KR = NT * HC
QPAD = SC + 16
HA, HB = 8, 4
TILES = B * NP // P
ALLT = TILES + 1
FIRST = ((0, 1), (1, 3), (3, KC))
EPS = 1e-5
SCALING = HD ** -0.5


def vit_block(nc, first_in, x_in, posb, w_qkv, w_out_in, bvo, cls_tok, w_node, small_in, out_patch, out_cls):
    fp32 = mybir.dt.float32
    ALU = mybir.AluOpType
    ACT = mybir.ActivationFunctionType
    AX = mybir.AxisListType

    v_scratch = nc.dram_tensor("v_scratch", (2, B, NP, C), fp32, kind="Internal").ap()
    vcls_scratch = nc.dram_tensor("vcls_scratch", (2, C), fp32, kind="Internal").ap()

    ctx = ExitStack()
    with ctx:
        def sb(name, shape):
            return ctx.enter_context(nc.sbuf_tensor(name, shape, fp32))

        def sem(name):
            return ctx.enter_context(nc.semaphore(name))

        first = sb("first", [P, KC, D + SB * NP])
        wtok = first[:, :, 0:D]
        wqkv = sb("wqkv", [C, 2, 3 * D])
        wout_in = sb("wout_in", [C, 2, D + NODES])
        wout, win = wout_in[:, :, 0:D], wout_in[:, :, D:]
        wnode = sb("wnode", [FEAT, D])
        pos = sb("pos", [P, 3, D])
        posbias = sb("posbias", [P, 2, D])
        small = sb("small", [P, P + 4 + HA + HC])
        ident, bqk, mask = small[:, 0:P], small[:, P:P + 4], small[:, P + 4:]
        bqs = sb("bqs", [P, 2])
        bvob = sb("bvob", [P, 2 * D])
        bvb, bob = bvob[:, 0:D], bvob[:, D:]
        mhalf = sb("mhalf", [P, 3])
        x_sb = sb("x_sb", [P, ST - 1, KC, SB * NP])
        patches = [first[:, :, D:]] + [x_sb[:, s - 1] for s in range(1, ST)]
        h = sb("h", [P, ALLT, D])
        hb = sb("hb", [P, ALLT, D])
        h2 = sb("h2", [P, ALLT, D])
        fin = sb("fin", [P, ALLT, D])
        hn = sb("hn", [P, 2, 2, D])
        h2n = sb("h2n", [P, 3, D])
        stats = sb("stats", [P, 3, 6])
        mv = sb("mv", [P, ALLT, 2])
        ve = sb("ve", [P, ALLT])
        rstd = sb("rstd", [P, ALLT])
        mv2 = sb("mv2", [P, ALLT, 2])
        ve2 = sb("ve2", [P, ALLT])
        rstd2 = sb("rstd2", [P, ALLT])
        hnT = sb("hnT", [C, 2, ST, NT, SB])
        qa = sb("qa", [P, ST, QPAD])
        qb = sb("qb", [64, ST, QPAD])
        bkm = sb("bkm", [64, HB])
        kda = sb("kda", [P, 2, HA, SC])
        kdb = sb("kdb", [64, 2, HB, SC])
        v_sb = sb("v_sb", [P, 2, 2, D])
        vcls = sb("vcls", [1, D])
        vc = sb("vc", [KR, 2, B, HD])
        vd = sb("vd", [KR, 2, 2, SB, C])
        smax = sb("smax", [P, 2, 24])
        dif = sb("dif", [P, 2, 2 * H * NT])
        ex = sb("ex", [P, 2, 4, KR])
        rsum = sb("rsum", [P, 2, 24])
        rinv = sb("rinv", [P, 2, 24])
        pT = sb("pT", [KR, 2, 4, P])
        att = sb("att", [P, 2, 2, D])
        oT = sb("oT", [C, 2, ST, NP, SB])
        oTc = sb("oTc", [C, 2, B])
        h2T = sb("h2T", [C, 2, 2, P])
        h2Tl = sb("h2Tl", [C, 2, 3, P])
        logit = sb("logit", [P, ALLT, NODES])
        gel = sb("gel", [P, ALLT, NODES])
        side = sb("side", [P, ALLT, NI, 2])
        path = sb("path", [P, ALLT, NODES])
        coef = sb("coef", [P, ALLT, FEAT])
        cT = sb("cT", [FEAT, ALLT, P])

        bank = [ctx.enter_context(nc.psum_tensor(f"bank{i}", [P, 512], fp32)) for i in range(8)]
        tokB = bank[0][:, 0:2 * D].rearrange("p (t d) -> p t d", t=2)
        embedB = [(bank[0][:, 0:D], bank[5][:, 0:D])] + [(b[:, 0:D], b[:, D:2 * D]) for b in (bank[6], bank[0], bank[7])]
        trB = bank[1]
        qaB, kaB, qkbB = bank[2], bank[3], bank[4]
        attB = [bank[2], bank[3]]
        oTB = [[bank[4], bank[7]], [bank[4], bank[7]], [bank[5], bank[6]], [bank[4], bank[7]]]
        scB = [bank[5], bank[6]]
        pTB = [bank[7], bank[4]]
        lgB = bank[1]
        lgB3 = bank[6]
        clsoB = bank[5]
        o3B = [bank[6], bank[0]]
        h2TB3 = [bank[3], bank[7]]
        coefB = [bank[3], bank[0], bank[3]]
        finB = [bank[2], bank[4], bank[5]]
        finB3 = {TILES: bank[6], 6: bank[1], 7: bank[7]}

        in_x = [None] + [sem(f"in_x{s}") for s in range(1, ST)]
        in_first = [sem(f"in_first{i}") for i in range(len(FIRST))]
        in_small, in_pos, in_cls, in_wqkv = sem("in_small"), sem("in_pos"), sem("in_cls"), sem("in_wqkv")
        in_bvo, in_wout, in_wnode = sem("in_bvo"), sem("in_wout"), sem("in_wnode")
        vcls_stored, v_stored = sem("vcls_stored"), sem("v_stored")
        vcls_back = sem("vcls_back")
        v_back = [sem(f"v_back{s}") for s in range(ST)]
        out_done = sem("out_done")
        pe_h, pe_hT, pe_qa, pe_ka = sem("pe_h"), sem("pe_hT"), sem("pe_qa"), sem("pe_ka")
        pe_qkb, pe_v, pe_sc, pe_pT = sem("pe_qkb"), sem("pe_v"), sem("pe_sc"), sem("pe_pT")
        pe_att, pe_oT, pe_o = sem("pe_att"), sem("pe_oT"), sem("pe_o")
        pe_h2T, pe_lg = sem("pe_h2T"), sem("pe_lg")
        pe_cT, pe_fin = sem("pe_cT"), sem("pe_fin")
        bqs_done, hT_copied, qa_copied, qb_copied = sem("bqs_done"), sem("hT_copied"), sem("qa_copied"), sem("qb_copied")
        kdb_ready, exp_done, pT_copied, oT_copied = sem("kdb_ready"), sem("exp_done"), sem("pT_copied"), sem("oT_copied")
        h2T_copied, lg_copied, gelu_done, cT_copied = sem("h2T_copied"), sem("lg_copied"), sem("gelu_done"), sem("cT_copied")
        h_added, ve_ready, hn_ready, v_added = sem("h_added"), sem("ve_ready"), sem("hn_ready"), sem("v_added")
        vcls_added, bkm_done, kda_ready, dif_ready = sem("vcls_added"), sem("bkm_done"), sem("kda_ready"), sem("dif_ready")
        sum_done, att_ready, h2_added, h2n_ready = sem("sum_done"), sem("att_ready"), sem("h2_added"), sem("h2n_ready")
        ve2_ready, h2T7_copied, sides_read = sem("ve2_ready"), sem("h2T7_copied"), sem("sides_read")
        coef_ready, fin_ready, dve_step = sem("coef_ready"), sem("fin_ready"), sem("dve_step")
        consts_set, rstd_ready, rstd2_ready = sem("consts_set"), sem("rstd_ready"), sem("rstd2_ready")
        vd_ready, hb_ready = sem("vd_ready"), sem("hb_ready")

        block = ctx.enter_context(nc.Block())

        def rows(t):
            return P if t < TILES else B

        @block.sync
        def _(sp):
            for (a, b), loaded in zip(FIRST, in_first):
                if b == KC:
                    sp.dma_start(h[0:B, TILES], cls_tok.to_broadcast([B, D])).then_inc(in_cls, 16)
                sp.dma_start(first[:, a:b], first_in[:, a:b]).then_inc(loaded, 16)
            sp.dma_start(small[:], small_in).then_inc(in_small, 16)
            sp.dma_start(x_sb[:, 0], x_in[0]).then_inc(in_x[1], 16)
            sp.dma_start(pos[:], posb).then_inc(in_pos, 16)
            sp.dma_start(wqkv[:], w_qkv).then_inc(in_wqkv, 16)
            sp.dma_start(x_sb[:, 1], x_in[1]).then_inc(in_x[2], 16)
            sp.dma_start(bvob[:], bvo.to_broadcast([P, 2 * D])).then_inc(in_bvo, 16)
            sp.dma_start(x_sb[:, 2], x_in[2]).then_inc(in_x[3], 16)
            sp.dma_start(wout_in[:], w_out_in).then_inc(in_wout, 16)
            sp.dma_start(wnode[:], w_node).then_inc(in_wnode, 16)
            sp.wait_ge(vcls_added, 1)
            sp.dma_start(vcls_scratch.rearrange("(a c) d -> a (c d)", a=1), vcls[:]).then_inc(vcls_stored, 16)
            sp.wait_ge(vcls_stored, 16)
            for c in range(2):
                src = vcls_scratch[c].rearrange("(h d) -> h d", d=HD).unsqueeze(1).to_broadcast([HC, B, HD])
                sp.dma_start(vc[0:HC, c], src).then_inc(vcls_back, 16)
            for s in range(ST):
                sp.wait_ge(v_added, s + 1)
                for t in range(2):
                    for c in range(2):
                        dst = v_scratch[c, s * SB:(s + 1) * SB, 8 * t:8 * t + 8].rearrange("b n d -> n b d")
                        sp.dma_start(dst, v_sb[:, s % 2, t, c * C:(c + 1) * C]).then_inc(v_stored, 16)
                sp.wait_ge(v_stored, 64 * (s + 1))
                for c in range(2):
                    src = v_scratch[c, s * SB:(s + 1) * SB].rearrange("b n (h d) -> (n h) b d", d=HD)
                    sp.dma_start(vc[HC:KR, c, s * SB:(s + 1) * SB], src).then_inc(v_back[s], 16)
            for g in range(3):
                sp.wait_ge(fin_ready, g + 1)
                sp.dma_start(out_patch[:, 2 * g:2 * g + 2], fin[:, 2 * g:2 * g + 2]).then_inc(out_done, 16)
            sp.wait_ge(fin_ready, 5)
            sp.dma_start(out_patch[:, 6:8], fin[:, 6:8]).then_inc(out_done, 16)
            sp.wait_ge(fin_ready, 6)
            sp.dma_start(out_cls, fin[0:B, TILES]).then_inc(out_done, 16)
            sp.wait_ge(out_done, 5 * 16)

        @block.gpsimd
        def _(pool):
            pool.memset(mhalf[:], -0.5).then_inc(consts_set, 1)
            pool.memset(qa[:, :, SC:], 0.0).then_inc(consts_set, 1)
            pool.memset(qb[:, :, SC:], 0.0).then_inc(consts_set, 1)
            pool.memset(h2Tl[:, :, 2, B:], 0.0).then_inc(consts_set, 1)
            pool.memset(coef[:, :, 0:1], 0.0).then_inc(consts_set, 1)

            def root(n, t0, nt, r):
                pool.wait_ge(ve_ready, n + 1)
                pool.tensor_tensor(rstd[0:r, t0:t0 + nt], ve[0:r, t0:t0 + nt], mhalf[0:r, 0:nt], ALU.pow).then_inc(rstd_ready, 1)

            def root2(s):
                pool.wait_ge(ve2_ready, s + 1)
                nt = 2 if s < ST - 1 else 3
                pool.tensor_tensor(rstd2[:, 2 * s:2 * s + nt], ve2[:, 2 * s:2 * s + nt], mhalf[:, 0:nt], ALU.pow).then_inc(rstd2_ready, 1)

            def add_bias_out(s):
                pool.wait_ge(h_added, s + 1)
                pool.tensor_tensor(hb[:, 2 * s:2 * s + 2], h[:, 2 * s:2 * s + 2], bob[:].unsqueeze(1).to_broadcast([P, 2, D]), ALU.add).then_inc(hb_ready, 1)

            def spread_values(s):
                if s == 0:
                    pool.wait_ge(vcls_back, 32)
                pool.wait_ge(v_back[s], 32)
                if s >= 2:
                    pool.wait_ge(pe_att, 2 * (s - 1))
                for c in range(2):
                    pool.tensor_tensor(vd[:, s % 2, c].rearrange("p b (h d) -> p b h d", d=HD),
                                       vc[:, c, s * SB:(s + 1) * SB].unsqueeze(2).to_broadcast([KR, SB, HC, HD]),
                                       mask[0:KR, HA:HA + HC].unsqueeze(1).unsqueeze(3).to_broadcast([KR, SB, HC, HD]),
                                       ALU.mult).then_inc(vd_ready, 1)

            pool.wait_ge(consts_set, 6)
            root(0, TILES, 1, B)
            root(1, 0, 2, P)
            pool.wait_ge(in_bvo, 16)
            pool.wait_ge(in_cls, 16)
            pool.tensor_tensor(hb[0:B, TILES], h[0:B, TILES], bob[0:B], ALU.add).then_inc(hb_ready, 1)
            root(2, 2, 2, P)
            add_bias_out(0)
            root(3, 4, 2, P)
            root(4, 6, 2, P)
            pool.wait_ge(in_small, 16)
            spread_values(0)
            spread_values(1)
            add_bias_out(1)
            for s in range(ST):
                if s < ST - 2:
                    spread_values(s + 2)
                root2(s)
                if s < ST - 2:
                    add_bias_out(s + 2)

        @block.scalar
        def _(sc):
            def copy_hT(s):
                sc.wait_ge(pe_hT, s + 2)
                if s >= 0:
                    src = trB[0:C, :].rearrange("p (c n b) -> p c n b", c=2, n=NP)
                    sc.activation(hnT[:, :, s, 1:NT], src, ACT.Copy).then_inc(hT_copied, 1)
                else:
                    sc.activation(hnT[:, :, :, 0], trB[0:C, 0:2 * B].rearrange("p (c s b) -> p c s b", c=2, s=ST), ACT.Copy).then_inc(hT_copied, 1)

            def by_image(ap):
                return ap.rearrange("p (n b) -> p b n", b=SB)

            def copy_qk(s):
                if s == 0:
                    sc.wait_ge(bqs_done, 1)
                    sc.wait_ge(bkm_done, 1)
                sc.wait_ge(pe_qkb, s + 1)
                if s >= 2:
                    sc.wait_ge(pe_sc, 2 * (s - 1))
                for n in range(HB):
                    last = sc.activation(kdb[:, s % 2, n], qkbB[64:P, 0:SC], ACT.Identity,
                                         bias=bkm[:, n:n + 1], scale=mask[0:64, n:n + 1])
                last.then_inc(kdb_ready, 1)
                sc.activation(qb[:, s, 0:SC].rearrange("p (b n) -> p b n", n=NT), by_image(qkbB[0:64, 0:SC]), ACT.Identity,
                              bias=bqs[0:64, 1:2], scale=SCALING).then_inc(qb_copied, 1)
                sc.wait_ge(pe_qa, s + 1)
                sc.activation(qa[:, s, 0:SC].rearrange("p (b n) -> p b n", n=NT), by_image(qaB[:, 0:SC]), ACT.Identity,
                              bias=bqs[:, 0:1], scale=SCALING).then_inc(qa_copied, 1)

            def exps(s, i):
                sc.wait_ge(dif_ready, 2 * s + i + 1)
                if s:
                    sc.wait_ge(sum_done, 2 * (s - 1) + i + 1)
                    sc.wait_ge(pe_pT, 2 * (s - 1) + i + 1)
                sc.activation(ex[:, i].rearrange("p g (k h) -> p g h k", h=HC),
                              dif[:, i].rearrange("p (g h k) -> p g h k", g=4, k=NT), ACT.Exp, bias=-1.0).then_inc(exp_done, 1)

            def copy_pT(s, i):
                sc.wait_ge(pe_pT, 2 * s + i + 1)
                if s:
                    sc.wait_ge(pe_att, 2 * (s - 1) + i + 1)
                sc.activation(pT[:, i], pTB[i][0:KR, :].rearrange("p (g q) -> p g q", g=4), ACT.Copy).then_inc(pT_copied, 1)

            def copy_oT(s):
                for i in range(2):
                    sc.wait_ge(pe_oT, 2 * s + 1 + i)
                    src = oTB[s][i][0:C, :].rearrange("p (c b q) -> p c b q", c=2, q=32)
                    sc.activation(oT[:, :, s, :, 8 * i:8 * i + 8].rearrange("p c n b -> p c b n"), src[:, :, :, 1:NT], ACT.Copy)
                    sc.activation(oTc[:, :, s * SB + 8 * i:s * SB + 8 * i + 8], src[:, :, :, 0], ACT.Copy).then_inc(oT_copied, 1)

            def copy_h2T(s):
                sc.wait_ge(pe_h2T, s + 1)
                if s:
                    sc.wait_ge(pe_lg, s)
                sc.activation(h2T[:, :, 0:2], trB[0:C, :].rearrange("p (c t q) -> p c t q", c=2, q=P), ACT.Copy).then_inc(h2T_copied, 1)

            def copy_logits(s):
                sc.wait_ge(pe_lg, s + 1)
                sc.wait_ge(rstd2_ready, s + 1)
                for t in range(2):
                    last = sc.activation(logit[:, 2 * s + t], lgB[:, t * NODES:(t + 1) * NODES], ACT.Copy, scale=rstd2[:, 2 * s + t:2 * s + t + 1])
                last.then_inc(lg_copied, 1)

            sc.wait_ge(in_small, 16)
            sc.activation(bqs[:], bqk[:].rearrange("p (a b) -> p b a", b=2)[:, 0], ACT.Copy, scale=SCALING).then_inc(bqs_done, 1)
            copy_hT(-1)
            copy_hT(0)
            copy_qk(0)
            copy_hT(1)
            copy_hT(2)
            exps(0, 0)
            copy_qk(1)
            exps(0, 1)
            for s in range(ST - 2):
                copy_pT(s, 0)
                copy_pT(s, 1)
                if s:
                    copy_h2T(s - 1)
                exps(s + 1, 0)
                if s:
                    copy_logits(s - 1)
                copy_oT(s)
                exps(s + 1, 1)
                if s + 3 < ST:
                    copy_hT(s + 3)
                copy_qk(s + 2)
            copy_pT(2, 0)
            copy_pT(2, 1)
            copy_h2T(1)
            exps(3, 0)
            exps(3, 1)
            copy_logits(1)
            copy_pT(3, 0)
            copy_pT(3, 1)
            copy_oT(2)

            def gelus(t0, t1):
                sc.wait_ge(lg_copied, t1 // 2)
                sc.activation(gel[:, t0:t1], logit[:, t0:t1], ACT.Gelu).then_inc(gelu_done, 1)

            gelus(0, 4)
            copy_oT(3)

            def copy_coef(i, t0, nt):
                sc.wait_ge(pe_cT, i + 1)
                sc.activation(cT[:, t0:t0 + nt], coefB[i][0:FEAT, 0:nt * P].rearrange("p (t q) -> p t q", q=P), ACT.Copy).then_inc(cT_copied, 1)

            copy_coef(0, 0, 4)
            copy_h2T(2)
            copy_logits(2)
            sc.wait_ge(pe_h2T, 4)
            sc.activation(h2Tl[:, :, 1:3].rearrange("p c t q -> p c (t q)")[:, :, 0:P + B],
                          h2TB3[0][0:C, :].rearrange("p (c q) -> p c q", c=2)[:, :, 0:P + B], ACT.Copy).then_inc(h2T_copied, 1)
            gelus(4, 6)
            sc.wait_ge(sides_read, 1)
            sc.wait_ge(rstd2_ready, ST)
            for t in range(6, ALLT):
                last = sc.activation(gel[:, t], lgB3[:, (t - 6) * NODES:(t - 5) * NODES], ACT.Gelu, scale=rstd2[:, t:t + 1])
            last.then_inc(gelu_done, 1)
            copy_coef(1, 4, 2)
            copy_coef(2, 6, 3)

        @block.vector
        def _(dve):
            steps = [0]

            def after(ins):
                steps[0] += 1
                ins.then_inc(dve_step, 1)
                dve.wait_ge(dve_step, steps[0])

            def moments(src, tiles, mv_, ve_, ve_sem):
                for i, t in enumerate(tiles):
                    r = rows(t)
                    last = dve.bn_stats(stats[0:r, i], src[0:r, t])
                after(last)
                for i, t in enumerate(tiles):
                    last = dve.bn_aggr(mv_[0:rows(t), t], stats[0:rows(t), i])
                after(last)
                rr = P if len(tiles) > 1 else rows(tiles[0])
                T = slice(tiles[0], tiles[-1] + 1)
                dve.tensor_scalar(ve_[0:rr, T], mv_[0:rr, T, 1], EPS, None, ALU.add).then_inc(ve_sem, 1)

            def layernorm1(tiles, rstd_at, dst, meanwhile=None):
                moments(h, tiles, mv, ve, ve_ready)
                if meanwhile:
                    meanwhile()
                dve.wait_ge(rstd_ready, rstd_at)
                for i, t in enumerate(tiles):
                    r = rows(t)
                    last = dve.tensor_scalar(dst[0:r, i], h[0:r, t], mv[0:r, t, 0:1], rstd[0:r, t:t + 1], ALU.subtract, ALU.mult)
                last.then_inc(hn_ready, 1)

            def embed(s, meanwhile=None):
                dve.wait_ge(pe_h, s + 1)
                if s == 0:
                    dve.tensor_tensor(h[:, 0], embedB[0][0], posbias[:, 0], ALU.add)
                    dve.tensor_tensor(h[:, 1], embedB[0][1], posbias[:, 1], ALU.add).then_inc(h_added, 1)
                else:
                    bk = (None, bank[6], bank[0], bank[7])[s]
                    dve.tensor_tensor(h[:, 2 * s:2 * s + 2], bk[:, 0:2 * D].rearrange("p (t d) -> p t d", t=2), posbias[:], ALU.add).then_inc(h_added, 1)
                dve.wait_ge(h_added, s + 1)
                if s >= 2:
                    dve.wait_ge(pe_hT, s)
                layernorm1((2 * s, 2 * s + 1), s + 2, hn[:, s % 2], meanwhile)

            def spread_keys(s):
                dve.wait_ge(pe_ka, s + 1)
                if s == 0:
                    dve.wait_ge(in_small, 16)
                if s >= 2:
                    dve.wait_ge(pe_sc, 2 * (s - 1))
                for hs in (0, HA // 2):
                    full = [P, HA // 2, SC]
                    dve.scalar_tensor_tensor(out=kda[:, s % 2, hs:hs + HA // 2],
                                             in0=kaB[:, 0:SC].unsqueeze(1).to_broadcast(full),
                                             scalar=bqk[:, 1:2],
                                             in1=mask[:, hs:hs + HA // 2].unsqueeze(2).to_broadcast(full),
                                             op0=ALU.add, op1=ALU.mult).then_inc(kda_ready, 1)

            def add_value_bias(s):
                dve.wait_ge(pe_v, s + 2)
                if s >= 2:
                    dve.wait_ge(v_stored, 64 * (s - 1))
                dve.tensor_tensor(v_sb[:, s % 2], trB[:, 0:2 * D].rearrange("p (t d) -> p t d", t=2),
                                  bvb[:].unsqueeze(1).to_broadcast([P, 2, D]), ALU.add).then_inc(v_added, 1)

            def shift_scores(s):
                for i in range(2):
                    dve.wait_ge(pe_sc, 2 * s + i + 1)
                    scores = scB[i][:, 0:2 * H * NT].rearrange("p (h k) -> p h k", k=NT)
                    after(dve.tensor_reduce(out=smax[:, i], in_=scores, axis=AX.X, op=ALU.max))
                    if s:
                        dve.wait_ge(exp_done, 2 * s + i - 1)
                    dve.scalar_tensor_tensor(out=dif[:, i].rearrange("p (h k) -> p h k", k=NT), in0=scores, scalar=1.0,
                                             in1=smax[:, i].unsqueeze(2).to_broadcast([P, 2 * H, NT]),
                                             op0=ALU.add, op1=ALU.subtract).then_inc(dif_ready, 1)

            def row_sums(s):
                for i in range(2):
                    dve.wait_ge(exp_done, 2 * s + i + 1)
                    dve.tensor_reduce(out=rsum[:, i], in_=ex[:, i].rearrange("p g (k h) -> p g h k", h=HC), axis=AX.X,
                                      op=ALU.add).then_inc(sum_done, 1)
                dve.wait_ge(sum_done, 2 * s + 2)
                after(dve.reciprocal(rinv[:], rsum[:]))

            def normalise(s):
                for i in range(2):
                    dve.wait_ge(pe_att, 2 * s + i + 1)
                    if s:
                        dve.wait_ge(pe_oT, 2 * (s - 1) + i + 1)
                    dve.tensor_tensor(att[:, i].rearrange("p g (h d) -> p (g h) d", d=HD),
                                      attB[i][:, 0:2 * D].rearrange("p (h d) -> p h d", d=HD),
                                      rinv[:, i].unsqueeze(2).to_broadcast([P, 2 * H, HD]), ALU.mult).then_inc(att_ready, 1)

            def residual(s):
                dve.wait_ge(pe_o, s + 1)
                dve.wait_ge(hb_ready, s + 2)
                dve.tensor_tensor(h2[:, 2 * s:2 * s + 2], tokB, hb[:, 2 * s:2 * s + 2], ALU.add).then_inc(h2_added, 1)
                dve.wait_ge(h2_added, s + 1)
                if s:
                    dve.wait_ge(pe_h2T, s)
                tiles = (2 * s, 2 * s + 1)
                moments(h2, tiles, mv2, ve2, ve2_ready)
                for i, t in enumerate(tiles):
                    r = rows(t)
                    last = dve.tensor_scalar(h2n[0:r, i], h2[0:r, t], mv2[0:r, t, 0:1], None, ALU.subtract)
                last.then_inc(h2n_ready, 1)

            def last_residual():
                dve.wait_ge(pe_o, ST)
                dve.wait_ge(hb_ready, ST + 1)
                dve.tensor_tensor(h2[0:B, TILES], clsoB[0:B, 0:D], hb[0:B, TILES], ALU.add).then_inc(h2_added, 1)
                dve.wait_ge(h2_added, ST)
                dve.bn_stats(stats[0:B, 2], h2[0:B, TILES])
                dve.wait_ge(pe_o, ST + 1)
                after(dve.tensor_tensor(h2[:, 6], o3B[0][:, 0:D], hb[:, 6], ALU.add))
                dve.bn_aggr(mv2[0:B, TILES], stats[0:B, 2])
                dve.bn_stats(stats[:, 0], h2[:, 6])
                dve.wait_ge(pe_o, ST + 2)
                after(dve.tensor_tensor(h2[:, 7], o3B[1][:, 0:D], hb[:, 7], ALU.add))
                dve.bn_aggr(mv2[:, 6], stats[:, 0]).then_inc(h2_added, 2)
                last = dve.bn_stats(stats[:, 1], h2[:, 7])

                def center(i, t):
                    r = rows(t)
                    dve.tensor_scalar(h2n[0:r, i], h2[0:r, t], mv2[0:r, t, 0:1], None, ALU.subtract).then_inc(h2n_ready, 1)

                dve.wait_ge(pe_h2T, ST - 1)
                center(2, TILES)
                after(last)
                after(dve.bn_aggr(mv2[:, 7], stats[:, 1]))
                center(0, 6)
                center(1, 7)
                dve.tensor_scalar(ve2[:, 6:ALLT], mv2[:, 6:ALLT, 1], EPS, None, ALU.add).then_inc(ve2_ready, 1)

            def tree_path(t0, nt, src):
                T = slice(t0, t0 + nt)
                dve.tensor_scalar(side[:, T, :, 0], src, 0.0, None, ALU.is_le)
                last = dve.tensor_scalar(side[:, T, :, 1], src, 0.0, None, ALU.is_gt)
                if nt == 3:
                    last.then_inc(sides_read, 1)
                    dve.wait_ge(sides_read, 1)
                else:
                    after(last)
                dve.tensor_copy(path[:, T, 1:3], side[:, T, 0])

                def down(parents, a, n):
                    return dve.tensor_tensor(path[:, T, 2 * a + 1:2 * (a + n) + 1].rearrange("p t (n e) -> p t n e", e=2),
                                             parents.unsqueeze(3).to_broadcast([P, nt, n, 2]),
                                             side[:, T, a:a + n], ALU.mult)
                after(down(side[:, T, 0], 1, 2))
                after(down(path[:, T, 3:7], 3, 4))
                after(down(path[:, T, 7:NI], 7, NI - 7))

            def tree_terms(t0, nt, gelus):
                T = slice(t0, t0 + nt)
                dve.wait_ge(gelu_done, gelus)
                dve.tensor_tensor(coef[:, T, 1:NODES].rearrange("p t (n e) -> p t n e", e=2),
                                  gel[:, T, 0:NI].unsqueeze(3).to_broadcast([P, nt, NI, 2]),
                                  path[:, T, 1:NODES].rearrange("p t (n e) -> p t n e", e=2), ALU.mult)
                own = NODES + NODES - 1 - NI
                last20 = gel[:, T, NODES - 1:NODES]
                dve.tensor_tensor(coef[:, T, NODES:own], path[:, T, NI:NODES - 1], gel[:, T, NI:NODES - 1], ALU.mult)
                dve.tensor_scalar(coef[:, T, own:own + 1], last20, 6.0, None, ALU.mult)
                dve.scalar_tensor_tensor(out=coef[:, T, own + 1:FEAT], in0=path[:, T, LEAF:NODES - 1], scalar=-1.0,
                                         in1=last20.to_broadcast([P, nt, NODES - 1 - LEAF]), op0=ALU.mult, op1=ALU.mult).then_inc(coef_ready, 1)

            dve.memset(mv2[B:P, TILES], 1.0).then_inc(consts_set, 1)
            dve.wait_ge(consts_set, 6)
            dve.wait_ge(in_cls, 16)
            layernorm1((TILES,), 1, hn[:, 1])
            dve.wait_ge(in_pos, 16)
            after(dve.tensor_tensor(posbias[:], pos[:, 0:2], pos[:, 2:3].to_broadcast([P, 2, D]), ALU.add))
            embed(0)
            dve.wait_ge(pe_v, 1)
            dve.wait_ge(in_bvo, 16)
            dve.tensor_tensor(vcls[:], bank[4][0:1, 0:D], bvb[0:1], ALU.add).then_inc(vcls_added, 1)
            dve.wait_ge(pe_hT, 1)
            embed(1)
            dve.wait_ge(in_small, 16)
            dve.tensor_scalar(bkm[:], mask[0:64, 0:HB], bqk[0:64, 3:4], None, ALU.mult).then_inc(bkm_done, 1)
            add_value_bias(0)
            spread_keys(0)
            embed(2)
            embed(3, meanwhile=lambda: add_value_bias(1))
            shift_scores(0)
            spread_keys(1)
            add_value_bias(2)
            row_sums(0)
            for s in range(ST - 2):
                normalise(s)
                shift_scores(s + 1)
                row_sums(s + 1)
                spread_keys(s + 2)
                residual(s)
                if s + 3 < ST:
                    add_value_bias(s + 3)
            shift_scores(3)
            normalise(2)
            row_sums(3)
            dve.wait_ge(lg_copied, 2)
            tree_path(0, 4, logit[:, 0:4, 0:NI])
            normalise(3)
            tree_terms(0, 4, 1)
            residual(2)
            last_residual()
            dve.wait_ge(pe_h2T, 5)
            dve.tensor_copy(h2Tl[:, :, 0], h2TB3[1][0:C, 0:2 * P].rearrange("p (c q) -> p c q", c=2)).then_inc(h2T7_copied, 1)
            dve.wait_ge(lg_copied, 3)
            tree_path(4, 2, logit[:, 4:6, 0:NI])
            tree_terms(4, 2, 2)
            dve.wait_ge(pe_lg, ST)
            tree_path(6, 3, lgB3[:, 0:3 * NODES].rearrange("p (t n) -> p t n", n=NODES)[:, :, 0:NI])
            tree_terms(6, 3, 3)
            for g in range(3):
                dve.wait_ge(pe_fin, g + 1)
                dve.tensor_tensor(fin[:, 2 * g:2 * g + 2], finB[g][:, 0:2 * D].rearrange("p (t d) -> p t d", t=2),
                                  h2[:, 2 * g:2 * g + 2], ALU.add).then_inc(fin_ready, 1)
            for i, t in enumerate((6, 7, TILES)):
                r = rows(t)
                dve.wait_ge(pe_fin, 4 + i)
                dve.tensor_tensor(fin[0:r, t], finB3[t][0:r, 0:D], h2[0:r, t], ALU.add).then_inc(fin_ready, 1)

        @block.tensor
        def _(pe):
            def project_patches(s):
                if s:
                    pe.wait_ge(in_x[s], 16)
                if s == 2:
                    pe.wait_ge(h_added, 1)
                if s == 0:
                    for k in range(KC):
                        for i, (a, b) in enumerate(FIRST):
                            if a == k:
                                pe.wait_ge(in_first[i], 16)
                        for t in range(2):
                            last = pe.matmul(embedB[s][t], patches[s][:, k, t * P:(t + 1) * P], wtok[:, k], start=(k == 0), stop=(k == KC - 1))
                else:
                    for t in range(2):
                        for k in range(KC):
                            last = pe.matmul(embedB[s][t], patches[s][:, k, t * P:(t + 1) * P], wtok[:, k], start=(k == 0), stop=(k == KC - 1))
                last.then_inc(pe_h, 1)

            def turn_hn(s):
                pe.wait_ge(hn_ready, s + 2)
                if s == 0:
                    pe.wait_ge(hT_copied, 1)
                else:
                    pe.wait_ge(v_added, s)
                for c in range(2):
                    for t in range(2):
                        last = pe.transpose(trB[0:C, (2 * c + t) * P:(2 * c + t + 1) * P], hn[:, s % 2, t, c * C:(c + 1) * C], ident[:])
                last.then_inc(pe_hT, 1)

            def values(s):
                pe.wait_ge(hT_copied, s + 2)
                for t in range(2):
                    for c in range(2):
                        last = pe.matmul(trB[:, t * D:(t + 1) * D], hnT[:, c, s, 1 + 8 * t:9 + 8 * t].rearrange("p n b -> p (n b)"), wqkv[:, c, 2 * D:3 * D],
                                         start=(c == 0), stop=(c == 1))
                last.then_inc(pe_v, 1)

            def queries_keys(s):
                pe.wait_ge(hT_copied, s + 2)
                if s == 0:
                    pe.wait_ge(in_wqkv, 16)
                parts = [(kaB, 1, pe_ka), (qkbB, 2, pe_qkb), (qaB, 0, pe_qa)]
                if s == 1:
                    parts[0:2] = [parts[1], parts[0]]
                for dst, col, done in parts:
                    if dst is qkbB:
                        if s == 0:
                            pe.wait_ge(vcls_added, 1)
                        elif s == 1:
                            pe.wait_ge(qb_copied, 1)
                        else:
                            pe.wait_ge(oT_copied, 2 * (s - 1) - 1)
                    elif s == 1:
                        pe.wait_ge(qa_copied, 1) if dst is qaB else pe.wait_ge(kda_ready, 2)
                    elif s:
                        pe.wait_ge(att_ready, 2 * (s - 1))
                    for c in range(2):
                        last = pe.matmul(dst[:, 0:SC], wqkv[:, c, col * P:(col + 1) * P],
                                         hnT[:, c, s].rearrange("p n b -> p (n b)"), start=(c == 0), stop=(c == 1))
                    last.then_inc(done, 1)

            def scores(s):
                pe.wait_ge(qa_copied, s + 1)
                pe.wait_ge(qb_copied, s + 1)
                pe.wait_ge(kda_ready, 2 * (s + 1))
                pe.wait_ge(kdb_ready, s + 1)
                if s == 0:
                    pe.wait_ge(consts_set, 6)
                    pe.wait_ge(h_added, 2)
                for g in range(4):
                    if g % 2 == 0 and s:
                        pe.wait_ge(dif_ready, 2 * s - 1 + g // 2)
                    by_image = [k[:, s % 2].rearrange("p h (n b) -> p h b n", b=SB) for k in (kda, kdb)]
                    for lo, hi, q, kd in ((0, HA, qa, by_image[0]), (HA, H, qb, by_image[1])):
                        for j in range(4):
                            b = 4 * g + j
                            col = (g % 2) * H * NT
                            last = pe.matmul(scB[g // 2][32 * j:32 * j + 32, col + lo * NT:col + hi * NT],
                                             q[:, s, b * NT:b * NT + 32], kd[:, :, b], start=True, stop=True)
                    if g % 2:
                        last.then_inc(pe_sc, 1)

            def turn_probs(s, i):
                pe.wait_ge(exp_done, 2 * s + i + 1)
                if s == ST - 1:
                    pe.wait_ge(pT_copied, 2 * s)
                elif i == 0 and s:
                    pe.wait_ge(oT_copied, 2 * s)
                elif i == 0:
                    pe.wait_ge(h_added, 4)
                else:
                    pe.wait_ge(qb_copied, s + 2)
                for g in range(4):
                    last = pe.transpose(pTB[i][0:KR, g * P:(g + 1) * P], ex[:, i, g], ident[:])
                last.then_inc(pe_pT, 1)

            def attend(s):
                if s < ST - 1:
                    pe.wait_ge(qa_copied, s + 2)
                    pe.wait_ge(kda_ready, 2 * (s + 2))
                else:
                    pe.wait_ge(att_ready, 2 * s)
                pe.wait_ge(vd_ready, 2 * (s + 1))
                for i in range(2):
                    pe.wait_ge(pT_copied, 2 * s + i + 1)
                    for g in range(2):
                        for c in range(2):
                            for j in range(4):
                                last = pe.matmul(attB[i][32 * j:32 * j + 32, (2 * g + c) * C:(2 * g + c + 1) * C],
                                                 pT[:, i, 2 * g + c, 32 * j:32 * j + 32], vd[:, s % 2, c, 8 * i + 4 * g + j],
                                                 start=True, stop=True)
                    last.then_inc(pe_att, 1)

            def turn_outputs(s):
                for i in range(2):
                    pe.wait_ge(att_ready, 2 * s + i + 1)
                    if s == 2:
                        pe.wait_ge(dif_ready, 2 * ST)
                    else:
                        pe.wait_ge(pT_copied, 2 * s + 2)
                    for c in range(2):
                        for g in range(2):
                            last = pe.transpose(oTB[s][i][0:C, (2 * c + g) * P:(2 * c + g + 1) * P], att[:, i, g, c * C:(c + 1) * C], ident[:])
                    last.then_inc(pe_oT, 1)

            def project_out(s):
                pe.wait_ge(oT_copied, 2 * (s + 1))
                if s == 0:
                    pe.wait_ge(in_wout, 16)
                    pe.wait_ge(h_added, 3)
                else:
                    pe.wait_ge(h2_added, s)
                for t in range(2):
                    for c in range(2):
                        last = pe.matmul(tokB[:, t], oT[:, c, s, 8 * t:8 * t + 8].rearrange("p n b -> p (n b)"), wout[:, c], start=(c == 0), stop=(c == 1))
                last.then_inc(pe_o, 1)

            def last_project_out():
                pe.wait_ge(oT_copied, 2 * ST)
                for c in range(2):
                    last = pe.matmul(clsoB[0:B, 0:D], oTc[:, c], wout[:, c], start=(c == 0), stop=(c == 1))
                last.then_inc(pe_o, 1)
                for t in range(2):
                    if t:
                        pe.wait_ge(h2_added, ST - 1)
                    for c in range(2):
                        last = pe.matmul(o3B[t][:, 0:D], oT[:, c, ST - 1, 8 * t:8 * t + 8].rearrange("p n b -> p (n b)"), wout[:, c], start=(c == 0), stop=(c == 1))
                    last.then_inc(pe_o, 1)

            def turn_h2n(s):
                pe.wait_ge(h2n_ready, s + 1)
                if s == 0:
                    pe.wait_ge(v_added, ST)
                else:
                    pe.wait_ge(lg_copied, s)
                for c in range(2):
                    for t in range(2):
                        last = pe.transpose(trB[0:C, (2 * c + t) * P:(2 * c + t + 1) * P], h2n[:, t, c * C:(c + 1) * C], ident[:])
                last.then_inc(pe_h2T, 1)

            def last_turn_h2n():
                for i, t, dst, col in ((2, TILES, h2TB3[0], P), (0, 6, h2TB3[0], 0), (1, 7, h2TB3[1], 0)):
                    pe.wait_ge(h2n_ready, ST + (0 if i == 2 else i + 1))
                    r, step = rows(t), P if i == 1 else 2 * P
                    for c in range(2):
                        last = pe.transpose(dst[0:C, c * step + col:c * step + col + r], h2n[0:r, i, c * C:(c + 1) * C], ident[0:r, 0:r])
                    if i < 2:
                        last.then_inc(pe_h2T, 1)

            def logits(s):
                pe.wait_ge(h2T_copied, s + 1)
                if s == 0:
                    pe.wait_ge(in_wout, 16)
                for t in range(2):
                    for c in range(2):
                        last = pe.matmul(lgB[:, t * NODES:(t + 1) * NODES], h2T[:, c, t], win[:, c], start=(c == 0), stop=(c == 1))
                last.then_inc(pe_lg, 1)

            def last_logits():
                for place, t in ((2, TILES), (1, 6), (0, 7)):
                    pe.wait_ge(h2T7_copied, 1) if t == 7 else pe.wait_ge(h2T_copied, ST)
                    for c in range(2):
                        last = pe.matmul(lgB3[:, (t - 6) * NODES:(t - 5) * NODES], h2Tl[:, c, place], win[:, c], start=(c == 0), stop=(c == 1))
                last.then_inc(pe_lg, 1)

            def turn_coef(b, tiles):
                for i, t in enumerate(tiles):
                    r = rows(t)
                    last = pe.transpose(coefB[b][0:FEAT, i * P:i * P + r], coef[0:r, t], ident[0:r, 0:r])
                last.then_inc(pe_cT, 1)

            def tree_out(g):
                for i, t in enumerate((2 * g, 2 * g + 1)):
                    last = pe.matmul(finB[g][:, i * D:(i + 1) * D], cT[:, t], wnode[:], start=True, stop=True)
                last.then_inc(pe_fin, 1)

            project_patches(0)
            pe.wait_ge(in_small, 16)
            pe.wait_ge(hn_ready, 1)
            for c in range(2):
                last = pe.transpose(trB[0:C, c * B:(c + 1) * B], hn[0:B, 1, 0, c * C:(c + 1) * C], ident[0:B, 0:B])
            last.then_inc(pe_hT, 1)
            project_patches(1)
            pe.wait_ge(hT_copied, 1)
            pe.wait_ge(in_wqkv, 16)
            for c in range(2):
                last = pe.matmul(bank[4][0:1, 0:D], hnT[:, c, 0, 0, 0:1], wqkv[:, c, 2 * D:3 * D], start=(c == 0), stop=(c == 1))
            last.then_inc(pe_v, 1)
            turn_hn(0)
            project_patches(2)
            values(0)
            queries_keys(0)
            turn_hn(1)
            project_patches(3)
            values(1)
            scores(0)
            turn_hn(2)
            queries_keys(1)
            turn_probs(0, 0)
            values(2)
            turn_probs(0, 1)
            for s in range(ST - 2):
                attend(s)
                if s:
                    turn_h2n(s - 1)
                scores(s + 1)
                if s:
                    logits(s - 1)
                turn_outputs(s)
                if s + 3 < ST:
                    turn_hn(s + 3)
                queries_keys(s + 2)
                project_out(s)
                turn_probs(s + 1, 0)
                turn_probs(s + 1, 1)
                if s + 3 < ST:
                    values(s + 3)
            scores(3)
            turn_h2n(1)
            attend(2)
            logits(1)
            turn_probs(3, 0)
            turn_probs(3, 1)
            turn_outputs(2)
            attend(3)
            project_out(2)
            turn_outputs(3)
            pe.wait_ge(coef_ready, 1)
            turn_coef(0, (0, 1, 2, 3))
            last_project_out()
            turn_h2n(2)
            pe.wait_ge(in_wnode, 16)
            pe.wait_ge(cT_copied, 1)
            tree_out(0)
            logits(2)
            last_turn_h2n()
            last_logits()
            tree_out(1)
            pe.wait_ge(coef_ready, 2)
            turn_coef(1, (4, 5))
            pe.wait_ge(coef_ready, 3)
            turn_coef(2, (6, 7, 8))
            pe.wait_ge(cT_copied, 2)
            tree_out(2)
            pe.wait_ge(cT_copied, 3)
            for t in (6, 7, TILES):
                r = rows(t)
                pe.matmul(finB3[t][0:r, 0:D], cT[:, t, 0:r], wnode[:], start=True, stop=True).then_inc(pe_fin, 1)


def kernel(**inputs):
    import numpy as _np
    import concourse.bacc as _bacc
    from concourse import mybir as _mybir
    from concourse.bass_utils import run_bass_kernel_spmd as _run

    a = {k: _np.asarray(v) for k, v in inputs.items()}
    xt = a["x"].reshape(ST, SB, 4, 16, 4, 16, 3).transpose(3, 5, 6, 0, 2, 4, 1).reshape(KC, P, ST, SB * NP)
    xt = _np.ascontiguousarray(xt.transpose(2, 1, 0, 3))
    w_tok = a["L0_tok_W"].reshape(KC, P, D).transpose(1, 0, 2)
    first = _np.concatenate([w_tok, xt[0]], 2)
    pos = _np.repeat(a["L0_tok_pos_emb"], SB, 0).reshape(2, P, D)
    posb = _np.stack([pos[0], pos[1], _np.tile(a["L0_tok_b"], (P, 1))], 1)
    wq, wk, wv = _np.split(a["L0_attn_w_qkv"], 3)
    bq, bk, bv = _np.split(a["L0_attn_b_qkv"], 3)
    w = _np.concatenate([wq[:P], wk[:P], wq[P:], wk[P:], wv])
    w_qkv = w.T.reshape(2, C, 3 * D).transpose(1, 0, 2)
    last64 = [_np.concatenate([b[P:], b[P:]]) for b in (bq, bk)]
    b_qkv = _np.stack([bq[:P], bk[:P], last64[0], last64[1]], 1)
    w_out = a["L0_attn_w_out"].T.reshape(2, C, D).transpose(1, 0, 2)
    w_in = a["L0_ffn_weights_in"].T.reshape(2, C, NODES).transpose(1, 0, 2)
    w_node = a["L0_ffn_weights_out"][_np.minimum(_np.arange(FEAT), NODES - 1)]
    masks = _np.zeros((P, HA + HC), _np.float32)
    masks[_np.arange(P), _np.arange(P) // HD] = 1.0
    masks[_np.arange(P), HA + _np.arange(P) % HC] = 1.0
    small = _np.concatenate([_np.eye(P, dtype=_np.float32), b_qkv, masks], 1)
    arrays = {
        "first_in": first, "x_in": xt[1:], "posb": posb, "w_qkv": w_qkv, "w_out_in": _np.concatenate([w_out, w_in], 2),
        "bvo": _np.concatenate([bv, a["L0_attn_b_out"]]).reshape(1, 2 * D), "cls_tok": a["cls_tok"].reshape(1, D),
        "w_node": w_node, "small_in": small,
    }
    arrays = {k: _np.ascontiguousarray(v) for k, v in arrays.items()}
    nc = _bacc.Bacc("TRN2", target_bir_lowering=False, num_devices=1)
    f32 = _mybir.dt.float32
    args = {k: nc.dram_tensor(k, v.shape, f32, kind="ExternalInput").ap() for k, v in arrays.items()}
    out_patch = nc.dram_tensor("out_patch", (P, TILES, D), f32, kind="ExternalOutput").ap()
    out_cls = nc.dram_tensor("out_cls", (B, D), f32, kind="ExternalOutput").ap()
    vit_block(nc, out_patch=out_patch, out_cls=out_cls, **args)
    r = _run(nc, [arrays], core_ids=[0])
    patch, cls = r.results[0]["out_patch"], r.results[0]["out_cls"]
    patch = patch.reshape(8, SB, ST, 2, D).transpose(2, 1, 3, 0, 4).reshape(B, NP, D)
    return _np.concatenate([cls[:, None, :], patch], 1)
```
